# Optimizing a Trainium2 kernel written in Bass

```python
import numpy as np
import jax
import jax.numpy as jnp

def _softmax(x, axis=-1):
    return jax.nn.softmax(x, axis=axis)

def _gelu(x):
    return jax.nn.gelu(x, approximate=True)

def _silu(x):
    return jax.nn.silu(x)

def _sigmoid(x):
    return jax.nn.sigmoid(x)

def _layernorm(x, axis=-1, eps=1e-05):
    m = jnp.mean(x, axis=axis, keepdims=True)
    v = jnp.var(x, axis=axis, keepdims=True)
    return (x - m) / jnp.sqrt(v + eps)

def _scatter_add(tgt, idx, src, axis=0):
    return tgt.at[idx].add(src)

def _segment_sum(src, seg, n):
    return jax.ops.segment_sum(src, seg, n)
kernel_name = 'mk_vit_tower_cls_d1_tok_img1024_r4_862aa5'

def setup_inputs(seed: int=0):
    np.random.seed(seed)
    _w = jnp.asarray

    def _rec_inputs():
        import jax
        import jax.numpy as jnp
        _rk = jax.random.key(seed)
        x = -0.000356955 + 1 * jax.random.normal(jax.random.fold_in(_rk, 1), (64, 3, 224, 224), jnp.float32)
        cls_tok = 0.02 * jax.random.normal(jax.random.fold_in(_rk, 5), (1, 1, 256), jnp.float32)
        return (x, cls_tok)
    x, cls_tok = _rec_inputs()

    def _L0_tok_setup():
        import jax, jax.numpy as jnp
        import numpy as np
        PATCH = 16
        H = W = 224
        C = 3
        NP_SIDE = H // PATCH
        NUM_PATCHES = NP_SIDE * NP_SIDE
        PATCH_DIM = C * PATCH * PATCH
        EMBED = 256
        key = jax.random.key(seed)
        k1, k2, k3, k4 = jax.random.split(key, 4)
        B = 128
        raw_pixels = jax.random.normal(k1, (B, C, H, W), dtype=jnp.float32)
        bound = 1.0 / np.sqrt(PATCH_DIM)
        W_embed = jax.random.uniform(k2, (PATCH_DIM, EMBED), minval=-bound, maxval=bound, dtype=jnp.float32)
        b_embed = jax.random.uniform(k3, (EMBED,), minval=-bound, maxval=bound, dtype=jnp.float32)
        pos_embed = jax.random.normal(k4, (1, NUM_PATCHES, EMBED), dtype=jnp.float32)
        return {'raw_pixels': raw_pixels, 'W_embed': W_embed, 'b_embed': b_embed, 'pos_embed': pos_embed}
    _L0_tok_all = _L0_tok_setup()
    _L0_tok_in = {k: v for k, v in _L0_tok_all.items() if k in ('W_embed', 'b_embed', 'pos_embed')}
    del _L0_tok_all

    def _L0_attn_setup():
        import jax, jax.numpy as jnp
        import numpy as np
        EMBED_DIM = 256
        N_HEADS = 16
        HEAD_DIM = EMBED_DIM // N_HEADS
        N_FEATURES = 64
        EPS = 0.0001

        def softmax_kernel(data, projection_matrix, eps=EPS):
            data_normalizer = data.shape[-1] ** (-0.25)
            proj = jnp.einsum('bhnd,fd->bhnf', data, projection_matrix) * data_normalizer
            proj_max = jnp.max(proj, axis=-1, keepdims=True)
            return jnp.exp(proj - proj_max + eps)
        key = jax.random.key(seed)
        k_x, k_w1, k_b1, k_w2, k_b2, k_p = jax.random.split(key, 6)
        B, N, D = (4, 1024, EMBED_DIM)
        s1 = 1.0 / np.sqrt(D)
        x = jax.random.normal(k_x, (B, N, D), dtype=jnp.float32)
        W_qkv = jax.random.uniform(k_w1, (3 * D, D), dtype=jnp.float32, minval=-s1, maxval=s1)
        b_qkv = jax.random.uniform(k_b1, (3 * D,), dtype=jnp.float32, minval=-s1, maxval=s1)
        W_proj = jax.random.uniform(k_w2, (D, D), dtype=jnp.float32, minval=-s1, maxval=s1)
        b_proj = jax.random.uniform(k_b2, (D,), dtype=jnp.float32, minval=-s1, maxval=s1)
        pm = jax.random.normal(k_p, (N_FEATURES, HEAD_DIM), dtype=jnp.float32)
        pm = pm / jnp.linalg.norm(pm, axis=-1, keepdims=True)
        return {'x': x, 'W_qkv': W_qkv, 'b_qkv': b_qkv, 'W_proj': W_proj, 'b_proj': b_proj, 'proj_mat': pm}
    _L0_attn_all = _L0_attn_setup()
    _L0_attn_in = {k: v for k, v in _L0_attn_all.items() if k in ('W_qkv', 'b_qkv', 'W_proj', 'b_proj', 'proj_mat')}
    del _L0_attn_all

    def _L0_ffn_setup():
        import jax, jax.numpy as jnp
        import numpy as np
        import math
        E = 32
        K = 2
        CF = 1.2
        D = 256
        F = 1024
        key = jax.random.key(seed)
        ks = jax.random.split(key, 7)
        s = 0.02
        return {'x': jax.random.normal(ks[0], (4, 512, D), jnp.float32), 'gate_w': jax.random.normal(ks[1], (D, E), jnp.float32) * s, 'gate_b': jnp.zeros((E,), jnp.float32), 'w1': jax.random.normal(ks[2], (E, D, F), jnp.float32) * s, 'b1': jnp.zeros((E, F), jnp.float32), 'w2': jax.random.normal(ks[3], (E, F, D), jnp.float32) * s, 'b2': jnp.zeros((E, D), jnp.float32)}
    _L0_ffn_all = _L0_ffn_setup()
    _L0_ffn_in = {k: v for k, v in _L0_ffn_all.items() if k in ('gate_w', 'gate_b', 'w1', 'b1', 'w2', 'b2')}
    del _L0_ffn_all
    return {'x': x, 'cls_tok': cls_tok, 'L0_tok_W_embed': _L0_tok_in['W_embed'], 'L0_tok_b_embed': _L0_tok_in['b_embed'], 'L0_tok_pos_embed': _L0_tok_in['pos_embed'], 'L0_attn_W_qkv': _L0_attn_in['W_qkv'], 'L0_attn_b_qkv': _L0_attn_in['b_qkv'], 'L0_attn_W_proj': _L0_attn_in['W_proj'], 'L0_attn_b_proj': _L0_attn_in['b_proj'], 'L0_attn_proj_mat': _L0_attn_in['proj_mat'], 'L0_ffn_gate_w': _L0_ffn_in['gate_w'], 'L0_ffn_gate_b': _L0_ffn_in['gate_b'], 'L0_ffn_w1': _L0_ffn_in['w1'], 'L0_ffn_b1': _L0_ffn_in['b1'], 'L0_ffn_w2': _L0_ffn_in['w2'], 'L0_ffn_b2': _L0_ffn_in['b2']}

def reference(x, cls_tok, L0_tok_W_embed, L0_tok_b_embed, L0_tok_pos_embed, L0_attn_W_qkv, L0_attn_b_qkv, L0_attn_W_proj, L0_attn_b_proj, L0_attn_proj_mat, L0_ffn_gate_w, L0_ffn_gate_b, L0_ffn_w1, L0_ffn_b1, L0_ffn_w2, L0_ffn_b2):
    import jax
    import jax.numpy as jnp

    def _L0_tok_ref(raw_pixels, W_embed, b_embed, pos_embed):
        import jax, jax.numpy as jnp
        import numpy as np
        PATCH = 16
        H = W = 224
        C = 3
        NP_SIDE = H // PATCH
        NUM_PATCHES = NP_SIDE * NP_SIDE
        PATCH_DIM = C * PATCH * PATCH
        EMBED = 256
        B = raw_pixels.shape[0]
        patches = raw_pixels.reshape(B, C, NP_SIDE, PATCH, NP_SIDE, PATCH)
        patches = patches.transpose(0, 2, 4, 1, 3, 5).reshape(B, NUM_PATCHES, PATCH_DIM)
        x = jnp.einsum('bnd,de->bne', patches, W_embed) + b_embed
        return x + pos_embed

    def _L0_attn_ref(x, W_qkv, b_qkv, W_proj, b_proj, proj_mat):
        import jax, jax.numpy as jnp
        import numpy as np
        EMBED_DIM = 256
        N_HEADS = 16
        HEAD_DIM = EMBED_DIM // N_HEADS
        N_FEATURES = 64
        EPS = 0.0001

        def softmax_kernel(data, projection_matrix, eps=EPS):
            data_normalizer = data.shape[-1] ** (-0.25)
            proj = jnp.einsum('bhnd,fd->bhnf', data, projection_matrix) * data_normalizer
            proj_max = jnp.max(proj, axis=-1, keepdims=True)
            return jnp.exp(proj - proj_max + eps)
        B, N, D = x.shape
        qkv = x @ W_qkv.T + b_qkv
        qkv = qkv.reshape(B, N, 3, N_HEADS, HEAD_DIM)
        qkv = jnp.transpose(qkv, (2, 0, 3, 1, 4))
        q, k, v = (qkv[0], qkv[1], qkv[2])
        q_prime = softmax_kernel(q, proj_mat)
        k_prime = softmax_kernel(k, proj_mat)
        kv = jnp.einsum('bhnf,bhnv->bhfv', k_prime, v)
        out = jnp.einsum('bhnf,bhfv->bhnv', q_prime, kv)
        k_sum = jnp.sum(k_prime, axis=2)
        normalizer = jnp.einsum('bhnf,bhf->bhn', q_prime, k_sum)[..., None]
        out = out / (normalizer + 1e-06)
        out = jnp.transpose(out, (0, 2, 1, 3)).reshape(B, N, D)
        return out @ W_proj.T + b_proj

    def _L0_ffn_ref(x, gate_w, gate_b, w1, b1, w2, b2):
        import jax, jax.numpy as jnp
        import numpy as np
        import math
        E = 32
        K = 2
        CF = 1.2
        D = 256
        F = 1024
        orig_shape = x.shape
        xt = x.reshape(-1, D)
        T = xt.shape[0]
        C = int(math.ceil(T * K / E * CF))
        logits = xt @ gate_w + gate_b
        probs = jax.nn.softmax(logits, axis=-1)
        top_w, top_i = jax.lax.top_k(probs, K)
        w = top_w / jnp.sum(top_w, axis=-1, keepdims=True)
        flat_e = top_i.reshape(-1)
        oh = jax.nn.one_hot(flat_e, E, dtype=jnp.int32)
        pos_all = jnp.cumsum(oh, axis=0) - 1
        pos = jnp.take_along_axis(pos_all, flat_e[:, None], axis=1)[:, 0]
        valid = pos < C
        pos_d = jnp.where(valid, pos, C)
        x_rep = jnp.repeat(xt, K, axis=0)
        xe = jnp.zeros((E, C, D), x.dtype).at[flat_e, pos_d].add(x_rep, mode='drop')
        he = jax.nn.gelu(jnp.einsum('ecd,edf->ecf', xe, w1) + b1[:, None, :], approximate=False)
        ye = jnp.einsum('ecf,efd->ecd', he, w2) + b2[:, None, :]
        y_flat = ye[flat_e, jnp.minimum(pos, C - 1)] * valid[:, None].astype(x.dtype)
        y = (y_flat.reshape(T, K, D) * w[..., None]).sum(axis=1)
        return y.reshape(orig_shape)
    h = _L0_tok_ref(x, L0_tok_W_embed, L0_tok_b_embed, L0_tok_pos_embed)
    h = jnp.concatenate([jnp.broadcast_to(cls_tok, (h.shape[0], 1, h.shape[2])), h], axis=1)
    h = h + _L0_attn_ref(_layernorm(h, axis=-1), L0_attn_W_qkv, L0_attn_b_qkv, L0_attn_W_proj, L0_attn_b_proj, L0_attn_proj_mat)
    h = h + _L0_ffn_ref(_layernorm(h, axis=-1), L0_ffn_gate_w, L0_ffn_gate_b, L0_ffn_w1, L0_ffn_b1, L0_ffn_w2, L0_ffn_b2)
    return h

_drawn_inputs = setup_inputs


def setup_inputs(seed=0):
    import zlib

    import numpy as np

    out = dict(_drawn_inputs(seed))
    spreads = {'L0_ffn_gate_b': (0.0, 0.1), 'L0_ffn_b1': (0.0, 0.404), 'L0_ffn_b2': (0.0, 0.1)}
    factors = {'cls_tok': 28.519, 'L0_attn_proj_mat': 8.0}
    for name, (base, spread) in spreads.items():
        noise = np.random.default_rng([zlib.crc32(name.encode()), seed]).standard_normal(out[name].shape)
        drawn = base * np.exp(spread * noise) if base else spread * noise
        out[name] = jnp.asarray(drawn.astype(out[name].dtype))
    for name, factor in factors.items():
        out[name] = (out[name] * factor).astype(out[name].dtype)
    return out
```

```python
from contextlib import ExitStack

import concourse.bass as bass
from concourse import mybir

F32 = mybir.dt.float32
F32R = mybir.dt.float32r
BF16 = mybir.dt.bfloat16
U32 = mybir.dt.uint32
ALU = mybir.AluOpType
ACT = mybir.ActivationFunctionType
AX_X = mybir.AxisListType.X

IMAGES, CHANNELS, SIDE, PATCH = 64, 3, 224, 16
GRID = SIDE // PATCH
PATCHES = GRID * GRID
TOKENS = PATCHES + 1
ROWS = IMAGES * TOKENS
D = 256
HEADS, HEAD, FEATS = 16, 16, 64
KCH = D // 128
PCH = CHANNELS * PATCH * PATCH // 128
GROUP = 8
GP = GROUP * GRID
TA = (TOKENS + 1) // 2
TB = TOKENS - TA
T2 = 2 * TA
PAIRS = HEADS // 2
KVW = 2 * HEAD + 2
EXPERTS, TOPK, HIDDEN = 32, 2, 1024
CAP = -(-int(ROWS * TOPK * 12) // (EXPERTS * 10))
TJ = 8
SP = -(-CAP // TJ)
SLOTS = SP * TJ
HALF = SLOTS // 2
FCH = HIDDEN // 128
ENTRY = 16
OUTSIDE = 65536.0
EPS = 1e-5
FEAT_EPS = 1e-4
DEN_EPS = 1e-6


class At:

    def __init__(self, base, c):
        self.known = c if base is None else None
        self.n = c if base is None else base * 2 + c
        self.half = c // 2 if base is None else base + c // 2
        self.par = c % 2


def inside(at):
    return at.known is None or 0 <= at.known < IMAGES


def wait(eng, sem, value, carrier=None):
    if isinstance(value, int):
        if value > 0:
            eng.wait_ge(sem, value)
        return
    eng.wait_ge(sem, value)
    if carrier is not None:
        eng.sem_inc(carrier, 1)


def capped(at, ahead, per=1):
    if at.known is None:
        return (at.n + ahead) * per
    return min(at.known + ahead, IMAGES) * per


def linker(eng, sem, base, carrier=None):
    count = [0]

    def link(ins):
        count[0] += 1
        ins.then_inc(sem, 1)
        wait(eng, sem, base + count[0], carrier)
    return link


def three(pe, out, w_hi, w_lo, x_hi, x_lo, start, stop):
    pe.matmul(out, w_hi, x_hi, start=start, stop=False)
    pe.matmul(out, w_hi, x_lo, start=False, stop=False)
    return pe.matmul(out, w_lo, x_hi, start=False, stop=stop)


def tower_kernel(nc, x, cls_tok, w_embed, b_embed, pos_embed, w_qkv, b_qkv, w_proj, b_proj,
                 proj_mat, gate_w, gate_b, w1, b1, w2, b2, out):
    h_rows = nc.dram_tensor("h_rows", [(IMAGES + 1) * TOKENS, D], F32, kind="Internal").ap()
    sum_rows = nc.dram_tensor("sum_rows", [ROWS + SLOTS, D], F32, kind="Internal").ap()
    x2_rows = nc.dram_tensor("x2_rows", [ROWS, D], F32, kind="Internal").ap()
    slot_table = nc.dram_tensor("slot_table", [EXPERTS * SLOTS, ENTRY], U32, kind="Internal").ap()

    with ExitStack() as ctx:
        def sb(name, shape, dt):
            return ctx.enter_context(nc.sbuf_tensor(name, shape, dt))

        ident = sb("ident", [128, 128], F32)
        b1_cols = sb("b1_cols", [128, EXPERTS, FCH], F32)
        keep = dict(ident=ident, b1_cols=b1_cols)
        with ExitStack() as attn_ctx:
            def ab(name, shape, dt):
                return attn_ctx.enter_context(nc.sbuf_tensor(name, shape, dt))

            keep.update(
                wqkv_hi=ab("wqkv_hi", [128, KCH, 3 * D], F32R), wqkv_lo=ab("wqkv_lo", [128, KCH, 3 * D], F32R),
                wp_hi=ab("wp_hi", [128, KCH, D], F32R), wp_lo=ab("wp_lo", [128, KCH, D], F32R),
                pb_hi=ab("pb_hi", [128, 512], F32R), pb_lo=ab("pb_lo", [128, 512], F32R),
                bqk=ab("bqk", [128, 4], F32), bv=ab("bv", [128, D], F32), bp=ab("bp", [128, D], F32),
                gw=ab("gw", [128, KCH, EXPERTS], F32), gb=ab("gb", [128, 2, EXPERTS], F32),
                before=ab("before", [TA, TA], BF16), ones=ab("ones", [TA, TA], BF16),
                kv_mask=ab("kv_mask", [128, KVW], F32), expert_no=ab("expert_no", [128, EXPERTS], F32),
                feat_eps=ab("feat_eps", [128, 1], F32), ln_eps=ab("ln_eps", [128, 1], F32))
            prepare(nc, keep, w_qkv, b_qkv, w_proj, b_proj, proj_mat, gate_w, gate_b, b1, cls_tok,
                    h_rows, slot_table, sum_rows)
            embed(nc, keep, x, w_embed, b_embed, pos_embed, h_rows)
            attend(nc, keep, h_rows, sum_rows, x2_rows, slot_table)
        experts(nc, keep, w1, w2, b2, x2_rows, sum_rows, slot_table)
        finish(nc, sum_rows, out)


def prepare(nc, keep, w_qkv, b_qkv, w_proj, b_proj, proj_mat, gate_w, gate_b, b1, cls_tok,
            h_rows, slot_table, sum_rows):
    ident, b1_cols = keep["ident"], keep["b1_cols"]
    QCH = 3 * D // 128
    with ExitStack() as ctx:
        def sb(name, shape, dt):
            return ctx.enter_context(nc.sbuf_tensor(name, shape, dt))

        def sem(name):
            return ctx.enter_context(nc.semaphore(name))

        wqkv_raw = sb("wqkv_raw", [128, QCH, D], F32)
        wp_raw = sb("wp_raw", [128, KCH, D], F32)
        pb_raw = sb("pb_raw", [128, 512], F32)
        b1_raw = sb("b1_raw", [EXPERTS, HIDDEN], F32)
        cls_sb = sb("cls_sb", [IMAGES + 1, D], F32)
        empty = sb("empty", [128, EXPERTS * SLOTS // 128 * ENTRY], F32)
        zero_rows = sb("zero_rows", [SP, TJ, D], F32)
        empty_u = sb("empty_u", [128, EXPERTS * SLOTS // 128 * ENTRY], U32)
        ps = [ctx.enter_context(nc.psum_tensor(f"prep_ps{i}", [128, 512], F32)) for i in range(5)]
        w_loaded, pb_zeroed, pb_loaded, cls_loaded, stored = (
            sem("w_loaded"), sem("pb_zeroed"), sem("pb_loaded"), sem("cls_loaded"), sem("prep_stored"))
        ident_zeroed, ident_ready, small = sem("ident_zeroed"), sem("ident_ready"), sem("small_step")
        turned, hi_ready, lo_ready, empty_ready, pool_step = (
            sem("turned"), sem("prep_hi"), sem("prep_lo"), sem("empty_ready"), sem("prep_pool_step"))
        block = ctx.enter_context(nc.Block())

        @block.sync
        def _(sp):
            sp.dma_start(wqkv_raw[:, :, :], w_qkv.rearrange("(m p) k -> p m k", p=128)).then_inc(w_loaded, 16)
            sp.dma_start(wp_raw[:, :, :], w_proj.rearrange("(m p) k -> p m k", p=128)).then_inc(w_loaded, 16)
            sp.dma_start(b1_raw[:, :], b1).then_inc(w_loaded, 16)
            sp.dma_start(keep["gw"][:, :, :], gate_w.rearrange("(k p) e -> p k e", p=128)).then_inc(w_loaded, 16)
            sp.dma_start(keep["bv"][:, :], b_qkv[2 * D:3 * D].partition_broadcast(128)).then_inc(w_loaded, 16)
            sp.dma_start(keep["bp"][:, :], b_proj.partition_broadcast(128)).then_inc(w_loaded, 16)
            for t in range(2):
                sp.dma_start(keep["gb"][:, t, :], gate_b.partition_broadcast(128)).then_inc(w_loaded, 16)
            with nc.allow_non_contiguous_dma(reason="512 biases, one a partition"):
                sp.dma_start(keep["bqk"][:, :], b_qkv[0:512].rearrange("(m p) -> p m", p=128)).then_inc(w_loaded, 16)
            sp.dma_start(cls_sb[:, :], cls_tok[0, 0, :].partition_broadcast(IMAGES + 1)).then_inc(cls_loaded, 16)
            sp.wait_ge(pb_zeroed, 1)
            with nc.allow_non_contiguous_dma(reason="64 x 16 projection, transposed, once a head"):
                for h in range(128 // HEAD):
                    sp.dma_start(pb_raw[h * HEAD:(h + 1) * HEAD, h * FEATS:(h + 1) * FEATS],
                                 proj_mat.rearrange("f d -> d f")).then_inc(pb_loaded, 16)
            sp.wait_ge(cls_loaded, 16)
            sp.dma_start(h_rows.rearrange("(i n) d -> i n d", n=TOKENS)[:, 0, :], cls_sb[:, :]).then_inc(stored, 16)
            sp.wait_ge(empty_ready, 1)
            sp.dma_start(slot_table.rearrange("(p s) w -> p (s w)", p=128), empty_u[:, :]).then_inc(stored, 16)
            sp.wait_ge(small, 9)
            sp.dma_start(sum_rows[ROWS:ROWS + SLOTS, :].rearrange("(p j) d -> p j d", j=TJ), zero_rows[:, :, :]).then_inc(stored, 16)
            sp.wait_ge(stored, 48)

        @block.gpsimd
        def _(pool):
            link = linker(pool, pool_step, 0)
            pool.memset(pb_raw[:, :], 0.0).then_inc(pb_zeroed, 1)
            pool.memset(ident[:, :], 0.0).then_inc(ident_zeroed, 1)
            pool.wait_ge(ident_zeroed, 1)
            pool.affine_select(out=ident[:, :], in_=ident[:, :], compare_op=ALU.not_equal, fill=1.0,
                               base=0, pattern=[[-1, 128]], channel_multiplier=1).then_inc(ident_ready, 1)
            pool.iota(keep["expert_no"][:, :], pattern=[[1, EXPERTS]], base=0, channel_multiplier=0,
                      allow_small_or_imprecise_dtypes=True).then_inc(small, 1)
            link(pool.memset(keep["ones"][:, :], 1.0))
            pool.affine_select(out=keep["before"][:, :], in_=keep["ones"][:, :], compare_op=ALU.is_gt, fill=0.0,
                               base=0, pattern=[[1, TA]], channel_multiplier=-1).then_inc(small, 1)
            pool.memset(keep["feat_eps"][:, :], FEAT_EPS).then_inc(small, 1)
            pool.memset(keep["ln_eps"][:, :], EPS).then_inc(small, 1)
            pool.memset(zero_rows[:, :, :], 0.0).then_inc(small, 1)
            link(pool.memset(keep["kv_mask"][:, :], 0.0))
            for p0, c0, c1 in ((0, 0, HEAD), (0, 2 * HEAD, 2 * HEAD + 1), (64, HEAD, 2 * HEAD), (64, 2 * HEAD + 1, KVW)):
                pool.memset(keep["kv_mask"][p0:p0 + 64, c0:c1], 1.0).then_inc(small, 1)
            pool.wait_ge(small, 9)

        @block.tensor
        def _(pe):
            pe.wait_ge(ident_ready, 1)
            pe.wait_ge(w_loaded, 16 * 9)
            for k in range(KCH):
                for m in range(QCH):
                    n = k * QCH + m
                    pe.transpose(ps[n // 4][:, n % 4 * 128:n % 4 * 128 + 128],
                                 wqkv_raw[:, m, k * 128:(k + 1) * 128], ident[:, :])
            for k in range(KCH):
                for m in range(KCH):
                    n = k * KCH + m
                    last = pe.transpose(ps[3][:, n * 128:n * 128 + 128],
                                        wp_raw[:, m, k * 128:(k + 1) * 128], ident[:, :])
            for c in range(FCH):
                last = pe.transpose(ps[4][:, c * EXPERTS:(c + 1) * EXPERTS], b1_raw[:, c * 128:(c + 1) * 128],
                                    ident[0:EXPERTS, 0:EXPERTS])
            last.then_inc(turned, 1)

        @block.scalar
        def _(act):
            act.wait_ge(turned, 1)
            for i in range(3):
                act.activation(keep["wqkv_hi"][:, :, :].rearrange("p k m -> p (k m)")[:, i * 512:(i + 1) * 512],
                               ps[i][:, :], ACT.Copy).then_inc(hi_ready, 1)
            act.activation(keep["wp_hi"][:, :, :].rearrange("p k m -> p (k m)"), ps[3][:, :], ACT.Copy).then_inc(hi_ready, 1)
            act.activation(b1_cols[:, :, :], ps[4][:, 0:FCH * EXPERTS].rearrange("p (c e) -> p e c", e=EXPERTS),
                           ACT.Copy).then_inc(hi_ready, 1)
            act.wait_ge(pb_loaded, 16 * 8)
            act.activation(keep["pb_hi"][:, :], pb_raw[:, :], ACT.Copy, scale=float(HEAD) ** -0.25).then_inc(hi_ready, 1)
            act.wait_ge(hi_ready, 6)

        @block.vector
        def _(dve):
            dve.memset(empty[:, :], 0.0).then_inc(lo_ready, 1)
            dve.wait_ge(lo_ready, 1)
            dve.memset(empty[:, :].rearrange("p (s w) -> p s w", w=ENTRY)[:, :, 0], float(ROWS + SLOTS)).then_inc(lo_ready, 1)
            dve.wait_ge(lo_ready, 2)
            dve.tensor_copy(empty_u[:, :], empty[:, :]).then_inc(empty_ready, 1)
            for i in range(4):
                dve.wait_ge(hi_ready, i + 1)
                hi = keep["wqkv_hi"] if i < 3 else keep["wp_hi"]
                lo = keep["wqkv_lo"] if i < 3 else keep["wp_lo"]
                at = slice(i % 3 * 512, i % 3 * 512 + 512)
                dve.tensor_tensor(lo[:, :, :].rearrange("p k m -> p (k m)")[:, at], ps[i][:, :],
                                  hi[:, :, :].bitcast(F32).rearrange("p k m -> p (k m)")[:, at],
                                  ALU.subtract).then_inc(lo_ready, 1)
            dve.wait_ge(hi_ready, 6)
            dve.scalar_tensor_tensor(keep["pb_lo"][:, :], pb_raw[:, :], float(HEAD) ** -0.25,
                                     keep["pb_hi"][:, :].bitcast(F32), ALU.mult, ALU.subtract).then_inc(lo_ready, 1)
            dve.wait_ge(lo_ready, 7)


def embed(nc, keep, x, w_embed, b_embed, pos_embed, h_rows):
    ident = keep["ident"]
    GROUPS = IMAGES // GROUP
    with ExitStack() as ctx:
        def sb(name, shape, dt):
            return ctx.enter_context(nc.sbuf_tensor(name, shape, dt))

        def sem(name):
            return ctx.enter_context(nc.semaphore(name))

        we_raw = sb("we_raw", [128, PCH, D], F32)
        we_hi, we_lo = sb("we_hi", [128, PCH, D], F32R), sb("we_lo", [128, PCH, D], F32R)
        pos_b = sb("pos_b", [GP, GRID, D], F32)
        be = sb("be", [GP, D], F32)
        raw = [sb(f"raw{p}", [GP, CHANNELS, PATCH * SIDE], F32) for p in range(2)]
        patch = [sb(f"patch{r}", [GP, PCH * 128], F32) for r in range(2)]
        xt_hi = [sb(f"xt_hi{r}", [128, PCH, GP], F32R) for r in range(2)]
        xt_lo = [sb(f"xt_lo{r}", [128, PCH, GP], F32R) for r in range(2)]
        h_out = [sb(f"h_out{p}", [GP, GRID, D], F32) for p in range(2)]
        xt_ps = [ctx.enter_context(nc.psum_tensor(f"xt_ps{r}", [128, 2, 512], F32)) for r in range(2)]
        h_ps = [ctx.enter_context(nc.psum_tensor(f"h_ps{r}", [GP, 512], F32)) for r in range(2)]
        w_loaded, w_hi, w_ready, pos_ready = sem("we_loaded"), sem("we_hi_done"), sem("we_ready"), sem("pos_ready")
        raw_loaded = [sem(f"raw_loaded{p}") for p in range(2)]
        regrouped = sem("regrouped")
        turned, hi_ready, lo_ready, h_summed, h_added, h_stored = (
            sem("xt_turned"), sem("xt_hi_ready"), sem("xt_lo_ready"), sem("h_summed"), sem("h_added"), [sem(f"h_stored{p}") for p in range(2)])
        waited = sem("waited")
        block = ctx.enter_context(nc.Block())
        UNITS = GRID

        def xt3(t):
            return t[:, :, :].rearrange("p (a b) t -> p a (b t)", a=2)

        @block.sync
        def _(sp):
            def load(g, p):
                for b in range(GROUP):
                    image = x[bass.ds(g * GROUP + b, 1), :, :, :] if not isinstance(g, int) else x[g * GROUP + b:g * GROUP + b + 1, :, :, :]
                    sp.dma_start(raw[p][b * GRID:(b + 1) * GRID, :, :],
                                 image.rearrange("a c (ph py) w -> (a ph) c (py w)", py=PATCH)).then_inc(raw_loaded[p], 16)

            sp.dma_start(we_raw[:, :, :], w_embed.rearrange("(j p) e -> p j e", p=128)).then_inc(w_loaded, 16)
            load(0, 0)
            sp.dma_start(be[:, :], b_embed.partition_broadcast(GP)).then_inc(w_loaded, 16)
            for b in range(GROUP):
                sp.dma_start(pos_b[b * GRID:(b + 1) * GRID, :, :],
                             pos_embed[0].rearrange("(ph pw) e -> ph pw e", pw=GRID)).then_inc(w_loaded, 16)
            load(1, 1)

            def store(g, p):
                wait(sp, h_added, g * UNITS + UNITS, waited)
                for b in range(GROUP):
                    row = (g * GROUP + b) * TOKENS + 1
                    dst = h_rows[bass.ds(row, PATCHES), :] if not isinstance(row, int) else h_rows[row:row + PATCHES, :]
                    sp.dma_start(dst.rearrange("(ph pw) e -> ph pw e", pw=GRID),
                                 h_out[p][b * GRID:(b + 1) * GRID, :, :]).then_inc(h_stored[p], 16)

            with sp.Fori(1, GROUPS // 2) as it:
                for p in range(2):
                    wait(sp, regrouped, it * (2 * UNITS) + (p - 1) * UNITS, waited)
                    load(it * 2 + p, p)
                    store(it * 2 + (p - 2), p)
            for p in range(2):
                store(GROUPS - 2 + p, p)
            for p in range(2):
                wait(sp, h_stored[p], 16 * GROUP * GROUPS // 2, waited)

        @block.gpsimd
        def _(pool):
            def group(g, half, p):
                wait(pool, raw_loaded[p], half * (16 * GROUP) + 16 * GROUP, waited)
                for w in range(GRID):
                    n = g * UNITS + w
                    wait(pool, turned, n - 1, waited)
                    pool.tensor_copy(patch[w % 2][:, :].rearrange("p (r x) -> p r x", x=PATCH),
                                     raw[p][:, :, :].rearrange("p c (y x) -> p (c y) x", x=SIDE)[:, :, w * PATCH:(w + 1) * PATCH])\
                        .then_inc(regrouped, 1)

            for p in range(2):
                group(p, 0, p)
            with pool.Fori(1, GROUPS // 2) as it:
                for p in range(2):
                    group(it * 2 + p, it, p)

        @block.tensor
        def _(pe):
            def turn(n, w):
                pe.wait_ge(regrouped, n + 1)
                wait(pe, lo_ready, n - 1)
                for j in range(PCH):
                    last = pe.transpose(xt_ps[w % 2][:, j // 3, j % 3 * GP:(j % 3 + 1) * GP],
                                        patch[w % 2][:, j * 128:(j + 1) * 128], ident[0:GP, 0:GP])
                last.then_inc(turned, 1)

            def product(n, w):
                pe.wait_ge(lo_ready, n + 1)
                wait(pe, h_added, n - 1)
                for j in range(PCH):
                    last = three(pe, h_ps[w % 2][:, 0:D], xt_hi[w % 2][:, j, :], xt_lo[w % 2][:, j, :],
                                 we_hi[:, j, :], we_lo[:, j, :], j == 0, j == PCH - 1)
                last.then_inc(h_summed, 1)

            def group(g):
                base = g * UNITS
                for w in range(GRID + 1):
                    if w < GRID:
                        turn(base + w, w)
                    if w > 0:
                        product(base + w - 1, w - 1)

            pe.wait_ge(w_ready, 1)
            group(0)
            with pe.Fori(1, GROUPS) as g:
                group(g)

        @block.scalar
        def _(act):
            act.wait_ge(w_loaded, 16 * (2 + GROUP))
            act.activation(we_hi[:, :, :], we_raw[:, :, :], ACT.Copy).then_inc(w_hi, 1)

            def group(g):
                for w in range(GRID):
                    n = g * UNITS + w
                    act.wait_ge(turned, n + 1)
                    wait(act, h_summed, n - 1)
                    act.activation(xt3(xt_hi[w % 2]), xt_ps[w % 2][:, :, 0:3 * GP], ACT.Copy).then_inc(hi_ready, 1)

            group(0)
            with act.Fori(1, GROUPS) as g:
                group(g)

        @block.vector
        def _(dve):
            dve.wait_ge(w_hi, 1)
            dve.tensor_tensor(we_lo[:, :, :], we_raw[:, :, :], we_hi[:, :, :].bitcast(F32), ALU.subtract).then_inc(w_ready, 1)
            dve.wait_ge(w_loaded, 16 * (2 + GROUP))
            dve.tensor_tensor(pos_b[:, :, :], pos_b[:, :, :], be[:, :].unsqueeze(1).to_broadcast([GP, GRID, D]),
                              ALU.add).then_inc(pos_ready, 1)
            dve.wait_ge(pos_ready, 1)

            def low(n, w):
                dve.wait_ge(hi_ready, n + 1)
                dve.tensor_tensor(xt3(xt_lo[w % 2]), xt_ps[w % 2][:, :, 0:3 * GP], xt3(xt_hi[w % 2]).bitcast(F32),
                                  ALU.subtract).then_inc(lo_ready, 1)

            def add(n, p, w):
                dve.wait_ge(h_summed, n + 1)
                dve.tensor_tensor(h_out[p][:, w, :], h_ps[w % 2][:, 0:D], pos_b[:, w, :], ALU.add).then_inc(h_added, 1)

            def group(g, half, p):
                base = g * UNITS
                for w in range(GRID + 1):
                    if w < GRID:
                        low(base + w, w)
                    if w == 1:
                        wait(dve, h_stored[p], half * (16 * GROUP))
                    if w > 0:
                        add(base + w - 1, p, w - 1)

            for p in range(2):
                group(p, 0, p)
            with dve.Fori(1, GROUPS // 2) as it:
                for p in range(2):
                    group(it * 2 + p, it, p)


def attend(nc, keep, h_rows, sum_rows, x2_rows, slot_table):
    ident = keep["ident"]
    wqkv_hi, wqkv_lo, wp_hi, wp_lo = keep["wqkv_hi"], keep["wqkv_lo"], keep["wp_hi"], keep["wp_lo"]
    pb_hi, pb_lo, bqk, bv, bp, gw, gb = (keep[k] for k in ("pb_hi", "pb_lo", "bqk", "bv", "bp", "gw", "gb"))
    before, ones, kv_mask, expert_no = keep["before"], keep["ones"], keep["kv_mask"], keep["expert_no"]
    feat_eps, ln_eps = keep["feat_eps"], keep["ln_eps"]
    with ExitStack() as ctx:
        def sb(name, shape, dt=F32):
            return ctx.enter_context(nc.sbuf_tensor(name, shape, dt))

        def two(name, shape, dt=F32):
            return [sb(f"{name}{p}", shape, dt) for p in range(2)]

        def sem(name):
            return ctx.enter_context(nc.semaphore(name))

        h_in, res = two("h_in", [TA, 2, D]), two("res", [TA, 2, D])
        xn, x2 = two("xn", [TA, 2, D]), two("x2", [TA, 2, D])
        mv1, mv2 = two("mv1_", [TA, 2, 2]), two("mv2_", [TA, 2, 2])
        lnv1, lnv2 = two("lnv1_", [TA, 2]), two("lnv2_", [TA, 2])
        y01, y02 = two("y01_", [TA, 2]), two("y02_", [TA, 2])
        hot, hot_sum, top_no = two("hot", [TA, 4, EXPERTS]), two("hot_sum", [TA, 2, EXPERTS], BF16), two("top_no", [TA, 2, 2])
        seen = two("seen", [TA, EXPERTS], BF16)
        gap, e_gap, rec_w = two("gap", [TA, 2]), two("e_gap", [TA, 2]), two("rec_w", [TA, 2])
        pos4, slot, entry = two("pos4_", [TA, 4]), two("slot", [TA, 4], U32), two("entry", [TA, 4, ENTRY], U32)
        stat1, stat2 = sb("stat1", [TA, 2, 6]), sb("stat2", [TA, 2, 6])
        ln_t = [sb(f"ln_t{i}", [TA, 2]) for i in range(3)]
        x_hi, x_lo = sb("x_hi", [128, KCH, T2], F32R), sb("x_lo", [128, KCH, T2], F32R)
        qk_hi, qk_lo = sb("qk_hi", [128, 4, T2], F32R), sb("qk_lo", [128, 4, T2], F32R)
        v_ext = sb("v_ext", [TA, 2, PAIRS, KVW])
        feat = [sb(f"feat{u}", [TA, HEADS, FEATS]) for u in range(4)]
        fmax = two("fmax", [TA, HEADS])
        kvb = sb("kvb", [128, PAIRS, KVW])
        qt = [sb(f"qt{j}", [128, 4, TA]) for j in range(4)]
        den, rec = sb("den", [TA, PAIRS, 2]), sb("rec", [TA, PAIRS, 2])
        attn = sb("attn", [TA, 2, D])
        a_hi, a_lo = sb("a_hi", [128, KCH, T2], F32R), sb("a_lo", [128, KCH, T2], F32R)
        x2t = sb("x2t", [128, KCH, T2])
        logit, top_v, top_i = sb("logit", [TA, 2, EXPERTS]), sb("top_v", [TA, 2, 8]), sb("top_i", [TA, 2, 8], U32)
        prod, den_w = sb("prod", [TA, 4, EXPERTS]), sb("den_w", [TA, 2])
        valid, e_w = sb("valid", [TA, 4]), sb("e_w", [TA, 2])
        slot_a, slot_b, slot_c = (sb(f"slot_{c}", [TA, 4]) for c in "abc")
        token_no = sb("token_no", [TA, 4])

        def bank(name, shape):
            return ctx.enter_context(nc.psum_tensor(name, shape, F32))

        f_ps = [bank(f"f_ps{t}", [TA, 2, 512]) for t in range(2)]
        bank4, bank5, bank6, bank7 = (bank(f"bank{i}", [128, 512]) for i in range(4, 8))

        h_loaded, res_loaded = [sem(f"h_loaded{p}") for p in range(2)], [sem(f"res_loaded{p}") for p in range(2)]
        h1_stored, x2_stored, slots_stored = ([sem(f"{n}{p}") for p in range(2)] for n in
                                              ("h1_stored", "x2_stored", "slots_stored"))
        set_up = sem("set_up")
        mv1_ready, mv2_ready, y01_ready, y02_ready, ln_act = (
            sem("mv1_ready"), sem("mv2_ready"), sem("y01_ready"), sem("y02_ready"), sem("ln_act_step"))
        xn_ready, x_turned, x_hi_ready, x_ready = sem("xn_ready"), sem("x_turned"), sem("x_hi_ready"), sem("x_ready")
        k_done, k_hi_ready, k_ready = sem("k_done"), sem("k_hi_ready"), sem("k_ready")
        q_done, q_hi_ready, q_ready = sem("q_done"), sem("q_hi_ready"), sem("q_ready")
        v_done, v_ready = sem("v_done"), sem("v_ready")
        feat_done, feat_maxed, feat_shifted, exp_done = sem("feat_done"), sem("feat_maxed"), sem("feat_shifted"), sem("exp_done")
        kv_done, kvb_ready, q_turned, qt_ready, o_done = sem("kv_done"), sem("kvb_ready"), sem("q_turned"), sem("qt_ready"), sem("o_done")
        norm_step, attn_ready, a_turned, a_hi_ready, a_ready = (
            sem("norm_step"), sem("attn_ready"), sem("a_turned"), sem("a_hi_ready"), sem("a_ready"))
        proj_done, res_ready, h1_ready, x2_ready, x2_turned, x2t_ready = (
            sem("proj_done"), sem("res_ready"), sem("h1_ready"), sem("x2_ready"), sem("x2_turned"), sem("x2t_ready"))
        gate_done, logit_ready, route_step, hot_ready, e_gap_ready = (
            sem("gate_done"), sem("logit_ready"), sem("route_step"), sem("hot_ready"), sem("e_gap_ready"))
        pos_done, pos_read, pos_step, rec_ready, slot_ready, wt_ready = (
            sem("pos_done"), sem("pos_read"), sem("pos_step"), sem("rec_ready"), sem("slot_ready"), sem("wt_ready"))
        ln1_dve, ln2_dve, seen_step = sem("ln1_dve_step"), sem("ln2_dve_step"), sem("seen_step")
        ln1_step, ln2_step, slot_step, stat1_step, stat2_step, tok_step = (
            sem("ln1_step"), sem("ln2_step"), sem("slot_step"), sem("stat1_step"), sem("stat2_step"), sem("tok_step"))
        waited = sem("waited")
        block = ctx.enter_context(nc.Block())

        FIRST, LOOP0, LOOP1, LAST = -2, 4, 62, IMAGES + 2

        def run(eng, pieces):
            def step(base, c):
                for piece, ahead in pieces:
                    at = At(base, c + ahead)
                    if inside(at):
                        piece(at)

            for s in range(FIRST, LOOP0):
                step(None, s)
            with eng.Fori(LOOP0 // 2, LOOP1 // 2) as it:
                for c in range(2):
                    step(it, c)
            for s in range(LOOP1, LAST):
                step(None, s)

        def rows(dram, at, first, count):
            if at.known is None:
                return dram[bass.ds(at.n * TOKENS + first, count), :]
            return dram[at.known * TOKENS + first:at.known * TOKENS + first + count, :]

        @block.sync
        def _(sp):
            def load_h(at):
                wait(sp, xn_ready, at.n - 1, waited)
                sp.dma_start(h_in[at.par][:, :, :], rows(h_rows, at, 0, T2).rearrange("(t p) d -> p t d", t=2))\
                    .then_inc(h_loaded[at.par], 16)

            def load_res(at):
                wait(sp, h1_stored[at.par], at.half * 32, waited)
                wait(sp, x2_ready, at.n - 1, waited)
                sp.dma_start(res[at.par][:, :, :], rows(h_rows, at, 0, T2).rearrange("(t p) d -> p t d", t=2))\
                    .then_inc(res_loaded[at.par], 16)

            def store_h1(at):
                wait(sp, h1_ready, at.n + 1, waited)
                for t, n in ((0, TA), (1, TB)):
                    sp.dma_start(rows(sum_rows, at, t * TA, n), res[at.par][0:n, t, :]).then_inc(h1_stored[at.par], 16)

            def store_x2(at):
                wait(sp, x2_ready, at.n + 1, waited)
                for t, n in ((0, TA), (1, TB)):
                    sp.dma_start(rows(x2_rows, at, t * TA, n), x2[at.par][0:n, t, :]).then_inc(x2_stored[at.par], 16)

            run(sp, [(load_h, 2), (load_res, 0), (store_h1, -1), (store_x2, -1)])
            for p in range(2):
                wait(sp, h1_stored[p], 32 * IMAGES // 2, waited)
                wait(sp, x2_stored[p], 32 * IMAGES // 2, waited)

        @block.gpsimd
        def _(pool):
            pool.iota(token_no[:, :], pattern=[[TA, 2], [0, 2]], base=0, channel_multiplier=1,
                      allow_small_or_imprecise_dtypes=True).then_inc(set_up, 1)
            pool.memset(v_ext[:, :, :, 2 * HEAD:KVW], 1.0).then_inc(set_up, 1)
            pool.memset(seen[0][:, :], 0.0).then_inc(set_up, 1)
            for p in range(2):
                pool.memset(entry[p][:, :, :].bitcast(F32), 0.0).then_inc(set_up, 1)
            wait(pool, set_up, 5)

            def norm(at, mv, y0, src, dst, step, ready):
                link = linker(pool, step, at.n * 5, waited)
                t0, t1, t2 = (t[:, :] for t in ln_t)
                link(pool.tensor_scalar(t0, mv[at.par][:, :, 1], EPS, None, ALU.add))
                link(pool.tensor_tensor(t1, y0[at.par][:, :], y0[at.par][:, :], ALU.mult))
                link(pool.tensor_tensor(t2, t1, t0, ALU.mult))
                link(pool.tensor_scalar(t1, t2, -0.5, 1.5, ALU.mult, ALU.add))
                link(pool.tensor_tensor(t2, t1, y0[at.par][:, :], ALU.mult))
                pool.tensor_scalar(dst[at.par][:, 0, :], src[at.par][:, 0, :], mv[at.par][:, 0, 0:1], t2[:, 0:1],
                                   ALU.subtract, ALU.mult)
                pool.tensor_scalar(dst[at.par][:, 1, :], src[at.par][:, 1, :], mv[at.par][:, 1, 0:1], t2[:, 1:2],
                                   ALU.subtract, ALU.mult).then_inc(ready, 1)

            def norm1(at):
                wait(pool, y01_ready, at.n + 1, waited)
                wait(pool, x_turned, at.n - 1, waited)
                norm(at, mv1, y01, h_in, xn, ln1_step, xn_ready)

            def norm2(at):
                wait(pool, y02_ready, at.n + 1, waited)
                wait(pool, x2_turned, at.n - 1, waited)
                wait(pool, x2_stored[at.par], at.half * 32, waited)
                norm(at, mv2, y02, res, x2, ln2_step, x2_ready)

            def add_bias(at):
                wait(pool, res_loaded[at.par], at.half * 16 + 16, waited)
                pool.tensor_tensor(res[at.par][:, :, :], res[at.par][:, :, :],
                                   bp[0:TA, :].unsqueeze(1).to_broadcast([TA, 2, D]), ALU.add).then_inc(res_ready, 1)

            def slots(at):
                link = linker(pool, slot_step, at.n * 7, waited)
                wait(pool, rec_ready, at.n + 1, waited)
                wait(pool, wt_ready, at.n, waited)
                wait(pool, slots_stored[at.par], at.half * 64, waited)
                link(pool.tensor_scalar(valid[:, :], pos4[at.par][:, :], float(CAP), None, ALU.is_lt))
                link(pool.tensor_scalar(slot_a[:, :], top_no[at.par][:, :, :].rearrange("p t k -> p (t k)"), float(SLOTS), None, ALU.mult))
                link(pool.tensor_tensor(slot_b[:, :], slot_a[:, :], pos4[at.par][:, :], ALU.add))
                link(pool.tensor_scalar(slot_a[:, :], valid[:, :], -OUTSIDE, OUTSIDE, ALU.mult, ALU.add))
                pool.tensor_copy(entry[at.par][:, :, 0], token_no[:, :])
                link(pool.tensor_tensor(slot_c[:, :], slot_a[:, :], slot_b[:, :], ALU.add))
                link(pool.tensor_copy(slot[at.par][:, :], slot_c[:, :]))
                wait(pool, e_gap_ready, at.n + 1, waited)
                pool.tensor_scalar(token_no[:, :], token_no[:, :], float(TOKENS), None, ALU.add)
                link(pool.tensor_tensor(e_w[:, :], e_gap[at.par][:, :], rec_w[at.par][:, :], ALU.mult))
                v = valid[:, :].rearrange("p (t k) -> p t k", k=2)
                w = entry[at.par][:, :, :].bitcast(F32).rearrange("p (t k) w -> p t k w", k=2)
                pool.tensor_tensor(w[:, :, 0, 1], rec_w[at.par][:, :], v[:, :, 0], ALU.mult)
                pool.tensor_tensor(w[:, :, 1, 1], e_w[:, :], v[:, :, 1], ALU.mult).then_inc(wt_ready, 1)
                wait(pool, wt_ready, at.n + 1, waited)
                for j in range(4):
                    n = TA if j < 2 else TB
                    pool.indirect_dma_start(slot_table, bass.IndirectOffsetOnAxis(slot[at.par][0:n, j:j + 1], 0),
                                            entry[at.par][0:n, j, :], None, bounds_check=EXPERTS * SLOTS - 1,
                                            oob_is_err=False).then_inc(slots_stored[at.par], 16)

            run(pool, [(add_bias, 0), (norm2, -1), (norm1, 2), (slots, -2)])
            for p in range(2):
                wait(pool, slots_stored[p], 64 * IMAGES // 2, waited)

        @block.tensor
        def _(pe):
            def features(at, u):
                t, q = u % 2, u // 2
                pe.wait_ge(q_ready if q else k_ready, at.n + 1)
                wait(pe, feat_shifted, at.n * 4 + u - 1)
                for c in range(2):
                    m = (0 if q else 2) + c
                    cols = slice(t * TA, (t + 1) * TA)
                    last = three(pe, f_ps[t][:, c, :], qk_hi[:, m, cols], qk_lo[:, m, cols], pb_hi[:, :], pb_lo[:, :], True, True)
                last.then_inc(feat_done, 1)

            def turn_x(at):
                pe.wait_ge(xn_ready, at.n + 1)
                wait(pe, qt_ready, at.n * 4 - 4)
                for k in range(KCH):
                    for t in range(2):
                        last = pe.transpose(bank4[:, (k * 2 + t) * TA:(k * 2 + t + 1) * TA],
                                            xn[at.par][:, t, k * 128:(k + 1) * 128], ident[0:TA, 0:TA])
                last.then_inc(x_turned, 1)

            def q_or_k(bank, m0, done):
                for c in range(2):
                    m = m0 + c
                    for k in range(KCH):
                        last = three(pe, bank[:, c * T2:(c + 1) * T2], wqkv_hi[:, k, m * 128:(m + 1) * 128],
                                     wqkv_lo[:, k, m * 128:(m + 1) * 128], x_hi[:, k, :], x_lo[:, k, :], k == 0, k == KCH - 1)
                last.then_inc(done, 1)

            def key(at):
                pe.wait_ge(x_ready, at.n + 1)
                q_or_k(bank4, 2, k_done)

            def query(at):
                wait(pe, h1_ready, at.n - 1)
                q_or_k(bank7, 0, q_done)

            def value(at):
                wait(pe, kvb_ready, at.n)
                for t in range(2):
                    for k in range(KCH):
                        cols = slice(t * TA, (t + 1) * TA)
                        last = three(pe, bank6[0:TA, t * D:(t + 1) * D], x_hi[:, k, cols], x_lo[:, k, cols],
                                     wqkv_hi[:, k, 2 * D:3 * D], wqkv_lo[:, k, 2 * D:3 * D], k == 0, k == KCH - 1)
                last.then_inc(v_done, 1)

            def key_value(at, t):
                pe.wait_ge(exp_done, at.n * 4 + t + 1)
                pe.wait_ge(v_ready, at.n + 1)
                wait(pe, attn_ready, at.n * 2 - 1)
                n = TB if t else TA
                for j in range(PAIRS):
                    last = pe.matmul(bank6[:, j * KVW:(j + 1) * KVW],
                                     feat[t][0:n, 2 * j:2 * j + 2, :].rearrange("p h f -> p (h f)"), v_ext[0:n, t, j, :],
                                     start=(t == 0 and j == 0), stop=(t == 1 and j == PAIRS - 1), skip_group_check=True)
                last.then_inc(kv_done, 1)

            def turn_q(at, j):
                t, half = j // 2, j % 2
                pe.wait_ge(exp_done, at.n * 4 + 3 + t)
                if half == 0:
                    wait(pe, x2t_ready, capped(at, 0))
                else:
                    wait(pe, k_ready, capped(at, 2))
                wait(pe, qt_ready, at.n * 4 + j - 1)
                bank = (bank5, bank4)[half]
                for i in range(4):
                    h = 8 * half + 2 * i
                    last = pe.transpose(bank[:, i * TA:(i + 1) * TA],
                                        feat[2 + t][:, h:h + 2, :].rearrange("p h f -> p (h f)"), ident[0:TA, 0:TA])
                last.then_inc(q_turned, 1)

            def output(at, t):
                pe.wait_ge(kvb_ready, at.n + 1)
                pe.wait_ge(qt_ready, at.n * 4 + 2 * t + 2)
                if t == 0:
                    pe.wait_ge(v_ready, capped(at, 2))
                else:
                    wait(pe, logit_ready, at.n)
                    pe.wait_ge(q_ready, capped(at, 2))
                bank = bank7 if t else bank6
                for j in range(PAIRS):
                    last = pe.matmul(bank[0:TA, j * KVW:(j + 1) * KVW], qt[2 * t + j // 4][:, j % 4, :], kvb[:, j, :],
                                     start=True, stop=True)
                last.then_inc(o_done, 1)

            def turn_a(at):
                pe.wait_ge(attn_ready, at.n * 2 + 2)
                pe.wait_ge(qt_ready, at.n * 4 + 3)
                for k in range(KCH):
                    for t in range(2):
                        last = pe.transpose(bank5[:, (k * 2 + t) * TA:(k * 2 + t + 1) * TA],
                                            attn[:, t, k * 128:(k + 1) * 128], ident[0:TA, 0:TA])
                last.then_inc(a_turned, 1)

            def project(at):
                pe.wait_ge(a_ready, at.n + 1)
                wait(pe, pos_read, at.n - 2)
                for t in range(2):
                    for k in range(KCH):
                        cols = slice(t * TA, (t + 1) * TA)
                        last = three(pe, bank7[0:TA, t * D:(t + 1) * D], a_hi[:, k, cols], a_lo[:, k, cols],
                                     wp_hi[:, k, :], wp_lo[:, k, :], k == 0, k == KCH - 1)
                last.then_inc(proj_done, 1)

            def turn_x2(at):
                pe.wait_ge(x2_ready, at.n + 1)
                pe.wait_ge(a_ready, at.n + 1)
                for k in range(KCH):
                    for t in range(2):
                        last = pe.transpose(bank5[:, (k * 2 + t) * TA:(k * 2 + t + 1) * TA],
                                            x2[at.par][:, t, k * 128:(k + 1) * 128], ident[0:TA, 0:TA])
                last.then_inc(x2_turned, 1)

            def gate(at):
                pe.wait_ge(x2t_ready, at.n + 1)
                wait(pe, pos_read, at.n)
                pe.wait_ge(q_ready, capped(at, 3))
                for t in range(2):
                    for k in range(KCH):
                        last = pe.matmul(bank7[0:TA, t * EXPERTS:(t + 1) * EXPERTS], x2t[:, k, t * TA:(t + 1) * TA],
                                         gw[:, k, :], start=(k == 0), stop=(k == KCH - 1))
                last.then_inc(gate_done, 1)

            def positions(at):
                pe.wait_ge(hot_ready, at.n + 1)
                pe.wait_ge(q_ready, capped(at, 4))
                pe.wait_ge(h1_ready, capped(at, 2))
                for t in range(2):
                    o = bank7[0:TA, t * EXPERTS:(t + 1) * EXPERTS]
                    pe.matmul(o, before[:, :], hot_sum[at.par][:, t, :], start=True, stop=False)
                    if t == 1:
                        pe.matmul(o, ones[:, :], hot_sum[at.par][:, 0, :], start=False, stop=False)
                    last = pe.matmul(o, ones[:, :], seen[at.par][:, :], start=False, stop=True)
                last.then_inc(pos_done, 1)

            pe.wait_ge(set_up, 5)
            run(pe, [(lambda at: features(at, 0), 0), (turn_a, -1), (lambda at: features(at, 1), 0), (turn_x, 1),
                     (project, -1), (lambda at: features(at, 2), 0), (lambda at: key_value(at, 0), 0), (key, 1),
                     (lambda at: features(at, 3), 0), (lambda at: key_value(at, 1), 0), (query, 1), (turn_x2, -1),
                     (value, 1), (positions, -2), (lambda at: turn_q(at, 0), 0), (lambda at: turn_q(at, 1), 0), (gate, -1),
                     (lambda at: output(at, 0), 0), (lambda at: turn_q(at, 2), 0), (lambda at: turn_q(at, 3), 0),
                     (lambda at: output(at, 1), 0)])

        @block.scalar
        def _(act):
            def rsqrt0(at, mv, lnv, y0, stats_ready, chain, ready):
                act.wait_ge(stats_ready, at.n + 1)
                act.activation(lnv[at.par][:, :], mv[at.par][:, :, 1], ACT.Ln, bias=ln_eps[0:TA, :]).then_inc(chain, 1)
                act.wait_ge(chain, at.n + 1)
                act.activation(y0[at.par][:, :], lnv[at.par][:, :], ACT.Exp, scale=-0.5).then_inc(ready, 1)

            def exp(at, u):
                act.wait_ge(feat_shifted, at.n * 4 + u + 1)
                f = feat[u][:, :, :].rearrange("p h f -> p (h f)")
                act.activation(f, f, ACT.Exp, bias=feat_eps[0:TA, :]).then_inc(exp_done, 1)

            def hi_x(at):
                act.wait_ge(x_turned, at.n + 1)
                wait(act, v_done, at.n)
                act.activation(x_hi[:, :, :].rearrange("p k t -> p (k t)"), bank4[:, 0:2 * T2], ACT.Copy).then_inc(x_hi_ready, 1)

            def hi_qk(at, bank, m0, done, ready):
                act.wait_ge(done, at.n + 1)
                wait(act, feat_done, at.n * 4 - (2 if m0 else 0))
                for c in range(2):
                    last = act.activation(qk_hi[:, m0 + c, :], bank[:, c * T2:(c + 1) * T2], ACT.Identity,
                                          bias=bqk[:, m0 + c:m0 + c + 1])
                last.then_inc(ready, 1)

            def copy_qt(at, j):
                act.wait_ge(q_turned, at.n * 4 + j + 1)
                wait(act, o_done, at.n * 2 - 1 + j // 2)
                act.activation(qt[j][:, :, :].rearrange("p i t -> p (i t)"), (bank5, bank4)[j % 2][:, 0:4 * TA],
                               ACT.Copy).then_inc(qt_ready, 1)

            def hi_a(at):
                act.wait_ge(a_turned, at.n + 1)
                wait(act, proj_done, at.n)
                act.activation(a_hi[:, :, :].rearrange("p k t -> p (k t)"), bank5[:, 0:2 * T2], ACT.Copy).then_inc(a_hi_ready, 1)

            def copy_x2t(at):
                act.wait_ge(x2_turned, at.n + 1)
                wait(act, gate_done, at.n)
                act.activation(x2t[:, :, :].rearrange("p k t -> p (k t)"), bank5[:, 0:2 * T2], ACT.Copy).then_inc(x2t_ready, 1)

            def exp_gap(at):
                act.wait_ge(hot_ready, at.n + 1)
                wait(act, wt_ready, at.n - 1)
                act.activation(e_gap[at.par][:, :], gap[at.par][:, :], ACT.Exp).then_inc(e_gap_ready, 1)

            act.preload_act_table_set("natural_log_exp_and_others")
            run(act, [(exp_gap, -2), (lambda at: exp(at, 0), 0), (hi_a, -1), (hi_x, 1), (lambda at: exp(at, 1), 0),
                      (lambda at: hi_qk(at, bank4, 2, k_done, k_hi_ready), 1), (lambda at: exp(at, 2), 0),
                      (lambda at: rsqrt0(at, mv2, lnv2, y02, mv2_ready, stat2_step, y02_ready), -1),
                      (lambda at: hi_qk(at, bank7, 0, q_done, q_hi_ready), 1), (lambda at: exp(at, 3), 0),
                      (copy_x2t, -1), (lambda at: copy_qt(at, 0), 0), (lambda at: copy_qt(at, 1), 0),
                      (lambda at: rsqrt0(at, mv1, lnv1, y01, mv1_ready, stat1_step, y01_ready), 2),
                      (lambda at: copy_qt(at, 2), 0), (lambda at: copy_qt(at, 3), 0)])

        @block.vector
        def _(dve):
            def statistics(at, src, stat, mv, step, ready):
                for t in range(2):
                    last = dve.bn_stats(stat[:, t, :], src[at.par][:, t, :])
                last.then_inc(step, 1)
                wait(dve, step, at.n + 1, waited)
                for t in range(2):
                    last = dve.bn_aggr(mv[at.par][:, t, :], stat[:, t, :])
                last.then_inc(ready, 1)

            def stats1(at):
                dve.wait_ge(h_loaded[at.par], at.half * 16 + 16)
                wait(dve, xn_ready, at.n - 1)
                statistics(at, h_in, stat1, mv1, ln1_dve, mv1_ready)

            def stats2(at):
                dve.wait_ge(h1_ready, at.n + 1)
                wait(dve, x2_ready, at.n - 1)
                statistics(at, res, stat2, mv2, ln2_dve, mv2_ready)

            def shift(at, u):
                dve.wait_ge(feat_done, at.n * 4 + u + 1)
                f = f_ps[u % 2][:, :, :].rearrange("p c (h f) -> p (c h) f", f=FEATS)
                dve.tensor_reduce(fmax[u % 2][:, :], f, AX_X, ALU.max).then_inc(feat_maxed, 1)
                if u < 2:
                    wait(dve, kv_done, at.n * 2 - 1 + u)
                else:
                    wait(dve, q_turned, at.n * 4 - 6 + 2 * u)
                dve.wait_ge(feat_maxed, at.n * 4 + u + 1)
                dve.tensor_tensor(feat[u][:, :, :], f, fmax[u % 2][:, :].unsqueeze(2).to_broadcast([TA, HEADS, FEATS]),
                                  ALU.subtract).then_inc(feat_shifted, 1)

            def lo_x(at):
                dve.wait_ge(x_hi_ready, at.n + 1)
                dve.tensor_tensor(x_lo[:, :, :].rearrange("p k t -> p (k t)"), bank4[:, 0:2 * T2],
                                  x_hi[:, :, :].bitcast(F32).rearrange("p k t -> p (k t)"), ALU.subtract).then_inc(x_ready, 1)

            def lo_qk(at, bank, m0, hi_ready, ready):
                dve.wait_ge(hi_ready, at.n + 1)
                for c in range(2):
                    last = dve.scalar_tensor_tensor(qk_lo[:, m0 + c, :], bank[:, c * T2:(c + 1) * T2], bqk[:, m0 + c:m0 + c + 1],
                                                    qk_hi[:, m0 + c, :].bitcast(F32), ALU.add, ALU.subtract)
                last.then_inc(ready, 1)

            def bias_v(at):
                dve.wait_ge(v_done, at.n + 1)
                wait(dve, kv_done, at.n * 2)
                for t in range(2):
                    last = dve.tensor_tensor(v_ext[:, t, :, 0:2 * HEAD],
                                             bank6[0:TA, t * D:(t + 1) * D].rearrange("p (j c) -> p j c", j=PAIRS),
                                             bv[0:TA, :].rearrange("p (j c) -> p j c", j=PAIRS), ALU.add)
                last.then_inc(v_ready, 1)

            def mask_kv(at):
                dve.wait_ge(kv_done, at.n * 2 + 2)
                wait(dve, o_done, at.n * 2)
                dve.tensor_tensor(kvb[:, :, :], bank6[:, 0:PAIRS * KVW].rearrange("p (j c) -> p j c", j=PAIRS),
                                  kv_mask[:, :].unsqueeze(1).to_broadcast([128, PAIRS, KVW]), ALU.mult).then_inc(kvb_ready, 1)

            def normalize(at, t):
                link = linker(dve, norm_step, at.n * 4 + 2 * t)
                dve.wait_ge(o_done, at.n * 2 + t + 1)
                wait(dve, a_turned, at.n)
                o = (bank7 if t else bank6)[0:TA, 0:PAIRS * KVW].rearrange("p (j c) -> p j c", j=PAIRS)
                link(dve.tensor_scalar(den[:, :, :], o[:, :, 2 * HEAD:KVW], DEN_EPS, None, ALU.add))
                link(dve.reciprocal(rec[:, :, :], den[:, :, :]))
                dve.tensor_tensor(attn[:, t, :].rearrange("p (j h d) -> p j h d", j=PAIRS, h=2),
                                  o[:, :, 0:2 * HEAD].rearrange("p j (h d) -> p j h d", h=2),
                                  rec[:, :, :].unsqueeze(3).to_broadcast([TA, PAIRS, 2, HEAD]), ALU.mult).then_inc(attn_ready, 1)

            def lo_a(at):
                dve.wait_ge(a_hi_ready, at.n + 1)
                dve.tensor_tensor(a_lo[:, :, :].rearrange("p k t -> p (k t)"), bank5[:, 0:2 * T2],
                                  a_hi[:, :, :].bitcast(F32).rearrange("p k t -> p (k t)"), ALU.subtract).then_inc(a_ready, 1)

            def residual(at):
                dve.wait_ge(proj_done, at.n + 1)
                dve.wait_ge(res_ready, at.n + 1)
                r = res[at.par][:, :, :].rearrange("p t d -> p (t d)")
                dve.tensor_tensor(r, bank7[0:TA, :], r, ALU.add).then_inc(h1_ready, 1)

            def route(at):
                link = linker(dve, route_step, at.n * 5, waited)
                dve.wait_ge(gate_done, at.n + 1)
                dve.tensor_tensor(logit[:, :, :], bank7[0:TA, 0:2 * EXPERTS].rearrange("p (t e) -> p t e", t=2),
                                  gb[0:TA, :, :], ALU.add).then_inc(logit_ready, 1)
                dve.wait_ge(logit_ready, at.n + 1)
                wait(dve, pos_done, at.n)
                wait(dve, wt_ready, at.n - 1)
                wait(dve, e_gap_ready, at.n - 1, waited)
                for t in range(2):
                    last = dve.max(top_v[:, t, :], logit[:, t, :])
                link(last)
                for t in range(2):
                    last = dve.max_index(top_i[:, t, :], top_v[:, t, :], logit[:, t, :])
                link(last)
                dve.tensor_tensor(gap[at.par][:, :], top_v[:, :, 1], top_v[:, :, 0], ALU.subtract)
                link(dve.tensor_copy(top_no[at.par][:, :, :], top_i[:, :, 0:2]))
                link(dve.tensor_tensor(hot[at.par][:, :, :], expert_no[0:TA, :].unsqueeze(1).to_broadcast([TA, 4, EXPERTS]),
                                       top_no[at.par][:, :, :].rearrange("p t k -> p (t k)").unsqueeze(2).to_broadcast([TA, 4, EXPERTS]),
                                       ALU.is_equal))
                h = hot[at.par][:, :, :].rearrange("p (t k) e -> p t k e", k=2)
                link(dve.tensor_tensor(hot_sum[at.par][:, :, :], h[:, :, 0, :], h[:, :, 1, :], ALU.add))
                s = seen[1 - at.par]
                dve.tensor_tensor(s[:, :], seen[at.par][:, :], hot_sum[at.par][:, 0, :], ALU.add).then_inc(seen_step, 1)
                dve.wait_ge(seen_step, at.n + 1)
                dve.tensor_tensor(s[0:TB, :], s[0:TB, :], hot_sum[at.par][0:TB, 1, :], ALU.add).then_inc(hot_ready, 1)

            def place(at):
                link = linker(dve, pos_step, at.n)
                dve.wait_ge(pos_done, at.n + 1)
                dve.wait_ge(hot_ready, at.n + 1)
                p = bank7[0:TA, 0:2 * EXPERTS].rearrange("p (t e) -> p t e", t=2)
                dve.tensor_tensor(prod[:, :, :].rearrange("p (t k) e -> p t k e", k=2),
                                  p.unsqueeze(2).to_broadcast([TA, 2, 2, EXPERTS]),
                                  hot[at.par][:, :, :].rearrange("p (t k) e -> p t k e", k=2), ALU.mult).then_inc(pos_read, 1)
                dve.wait_ge(pos_read, at.n + 1)
                wait(dve, wt_ready, at.n - 1)
                dve.wait_ge(e_gap_ready, at.n + 1)
                link(dve.tensor_scalar(den_w[:, :], e_gap[at.par][:, :], 1.0, None, ALU.add))
                dve.tensor_reduce(pos4[at.par][:, :], prod[:, :, :], AX_X, ALU.add)
                dve.reciprocal(rec_w[at.par][:, :], den_w[:, :]).then_inc(rec_ready, 1)

            dve.wait_ge(set_up, 5)
            run(dve, [(lambda at: shift(at, 0), 0), (lo_a, -1), (lambda at: shift(at, 1), 0), (lo_x, 1), (residual, -1),
                      (stats2, -1), (lambda at: shift(at, 2), 0), (lambda at: lo_qk(at, bank4, 2, k_hi_ready, k_ready), 1),
                      (lambda at: shift(at, 3), 0), (mask_kv, 0), (stats1, 2),
                      (lambda at: lo_qk(at, bank7, 0, q_hi_ready, q_ready), 1), (bias_v, 1), (place, -2), (route, -1),
                      (lambda at: normalize(at, 0), 0), (lambda at: normalize(at, 1), 0)])


def experts(nc, keep, w1, w2, b2, x2_rows, sum_rows, slot_table):
    ident, b1_cols = keep["ident"], keep["b1_cols"]
    CH = 2 * FCH
    with ExitStack() as ctx:
        def sb(name, shape, dt=F32):
            return ctx.enter_context(nc.sbuf_tensor(name, shape, dt))

        def sem(name):
            return ctx.enter_context(nc.semaphore(name))

        w1_raw, w2_raw = sb("w1_raw", [128, KCH, HIDDEN]), sb("w2_raw", [128, FCH, D])
        w1_hi, w1_lo = sb("w1_hi", [128, KCH, HIDDEN], F32R), sb("w1_lo", [128, KCH, HIDDEN], F32R)
        w2_hi, w2_lo = sb("w2_hi", [128, FCH, D], F32R), sb("w2_lo", [128, FCH, D], F32R)
        b2_row = sb("b2_row", [SP, D])
        b1_col = [sb(f"b1_col{p}", [128, FCH]) for p in range(2)]
        entries = sb("entries", [SP, TJ, ENTRY], U32)
        token, source = sb("token", [SP, TJ]), sb("source", [SP, TJ], U32)
        target = [sb(f"target{p}", [SP, TJ], U32) for p in range(2)]
        spare = sb("spare", [SP, TJ])
        weight = [sb(f"weight{p}", [SP, TJ]) for p in range(2)]
        xe = sb("xe", [SP, TJ, D])
        xe_hi, xe_lo = sb("xe_hi", [128, KCH, SLOTS], F32R), sb("xe_lo", [128, KCH, SLOTS], F32R)
        act_out = [sb(f"act_out{r}", [128, HALF]) for r in range(4)]
        he_hi, he_lo = sb("he_hi", [128, 2, FCH, HALF], F32R), sb("he_lo", [128, 2, FCH, HALF], F32R)
        y_bias = [sb(f"y_bias{r}", [SP, 2, D]) for r in range(2)]
        y_sb = sb("y_sb", [SP, TJ, D])
        u_ps = [ctx.enter_context(nc.psum_tensor(f"u_ps{r}", [128, 512], F32)) for r in range(4)]
        y_ps = [ctx.enter_context(nc.psum_tensor(f"y_ps{r}", [SP, 2, D], F32)) for r in range(2)]
        x_ps = [ctx.enter_context(nc.psum_tensor(f"x_ps{r}", [128, 512], F32)) for r in range(2)]

        w1_loaded, w2_loaded, b2_loaded, table_loaded = sem("w1_loaded"), sem("w2_loaded"), sem("b2_loaded"), sem("table_loaded")
        w1_hi_ready, w1_ready, w2_hi_ready, w2_ready = sem("w1_hi_ready"), sem("w1_ready"), sem("w2_hi_ready"), sem("w2_ready")
        index_step, source_ready, gathered, scattered = sem("index_step"), sem("source_ready"), sem("gathered"), sem("scattered")
        xe_turned, xe_hi_ready, xe_ready = sem("xe_turned"), sem("xe_hi_ready"), sem("xe_ready")
        b1_ready, up_done, gelu_done, he_hi_done, he_ready = (
            sem("b1_ready"), sem("up_done"), sem("gelu_done"), sem("he_hi_done"), sem("he_ready"))
        down_done, y_biased, y_ready, spare_ready = sem("down_done"), sem("y_biased"), sem("y_ready"), sem("spare_ready")
        waited = sem("waited")
        block = ctx.enter_context(nc.Block())

        def of(dram, e):
            return dram[e] if isinstance(e, int) else dram[bass.ds(e, 1)]

        def run(eng, first, turn):
            first()
            for e in range(2):
                turn(e, e, True)
            with eng.Fori(1, EXPERTS // 2 - 1) as it:
                for p in range(2):
                    turn(it * 2 + p, p, True)
            turn(EXPERTS - 2, 0, True)
            turn(EXPERTS - 1, 1, False)

        w1_v = w1.rearrange("e (k p) f -> e p k f", p=128)
        w2_v = w2.rearrange("e (c p) d -> e p c d", p=128)
        table_v = slot_table.rearrange("(e p j) w -> e p j w", p=SP, j=TJ)

        @block.sync
        def _(sp):
            def squeeze(ap, e):
                return ap if isinstance(e, int) else ap.rearrange("a p k f -> (a p) k f")

            def load_w1(e):
                wait(sp, w1_ready, e * 2, waited)
                sp.dma_start(w1_raw[:, :, :], squeeze(of(w1_v, e), e)).then_inc(w1_loaded, 16)

            def load_w2(e):
                wait(sp, w2_ready, e * 2, waited)
                sp.dma_start(w2_raw[:, :, :], squeeze(of(w2_v, e), e)).then_inc(w2_loaded, 16)

            def load_table(e):
                wait(sp, source_ready, e, waited)
                sp.dma_start(entries[:, :, :], squeeze(of(table_v, e), e)).then_inc(table_loaded, 16)

            def load_b2(e):
                wait(sp, y_biased, e * 4, waited)
                row = b2[e] if isinstance(e, int) else b2[bass.ds(e, 1), :].rearrange("a d -> (a d)")
                sp.dma_start(b2_row[:, :], row.partition_broadcast(SP)).then_inc(b2_loaded, 16)

            def first():
                load_table(0)
                load_w1(0)
                load_w2(0)

            def turn(e, p, more):
                load_b2(e)
                if more:
                    load_w1(e + 1)
                    load_table(e + 1)
                    load_w2(e + 1)

            run(sp, first, turn)

        @block.gpsimd
        def _(pool):
            def gather(e):
                wait(pool, source_ready, e + 1, waited)
                wait(pool, xe_turned, e * 4, waited)
                for j in range(TJ):
                    pool.indirect_dma_start(xe[:, j, :], None, x2_rows, bass.IndirectOffsetOnAxis(source[:, j:j + 1], 0))\
                        .then_inc(gathered, 16)

            def scatter(e, p):
                wait(pool, scattered, e * (16 * TJ), waited)
                for j in range(TJ):
                    if j % 2 == 0:
                        wait(pool, y_ready, e * 4 + j // 2 + 1, waited)
                    pool.indirect_dma_start(sum_rows, bass.IndirectOffsetOnAxis(target[p][:, j:j + 1], 0), y_sb[:, j, :], None,
                                            compute_op=ALU.add).then_inc(scattered, 16)

            def turn(e, p, more):
                if more:
                    gather(e + 1)
                scatter(e, p)

            pool.iota(spare[:, :], pattern=[[1, TJ]], base=ROWS, channel_multiplier=TJ,
                      allow_small_or_imprecise_dtypes=True).then_inc(spare_ready, 1)
            run(pool, lambda: gather(0), turn)
            wait(pool, scattered, EXPERTS * TJ * 16, waited)

        @block.tensor
        def _(pe):
            def turn_x(e, i):
                half, k = i // 2, i % 2
                if i == 0:
                    pe.wait_ge(gathered, e * (16 * TJ) + 16 * TJ)
                wait(pe, xe_ready, e * 4 + i - 1)
                for j in range(4):
                    last = pe.transpose(x_ps[i % 2][:, j * SP:(j + 1) * SP], xe[:, half * 4 + j, k * 128:(k + 1) * 128],
                                        ident[0:SP, 0:SP])
                last.then_inc(xe_turned, 1)

            def up(e, i):
                half, c = i // FCH, i % FCH
                if i == 0:
                    pe.wait_ge(w1_ready, e * 2 + 2)
                if c == 0:
                    pe.wait_ge(xe_ready, e * 4 + 2 * half + 2)
                wait(pe, gelu_done, e * CH + i - 3)
                for k in range(KCH):
                    last = three(pe, u_ps[i % 4][:, 0:HALF], w1_hi[:, k, c * 128:(c + 1) * 128],
                                 w1_lo[:, k, c * 128:(c + 1) * 128], xe_hi[:, k, half * HALF:(half + 1) * HALF],
                                 xe_lo[:, k, half * HALF:(half + 1) * HALF], k == 0, k == KCH - 1)
                last.then_inc(up_done, 1)

            def down(e, i):
                half = i // 2
                if i == 0:
                    pe.wait_ge(w2_ready, e * 2 + 2)
                if i % 2 == 0:
                    pe.wait_ge(he_ready, e * CH + (half + 1) * FCH)
                wait(pe, y_biased, e * 4 + i - 1)
                for j in range(2):
                    cols = slice((i % 2 * 2 + j) * SP, (i % 2 * 2 + j + 1) * SP)
                    for c in range(FCH):
                        last = three(pe, y_ps[i % 2][:, j, :], he_hi[:, half, c, cols], he_lo[:, half, c, cols],
                                     w2_hi[:, c, :], w2_lo[:, c, :], c == 0, c == FCH - 1)
                last.then_inc(down_done, 1)

            def turn(e, p, more):
                for i in range(CH):
                    up(e, i)
                for i in range(4):
                    down(e, i)
                    if more and i < 2:
                        turn_x(e + 1, 2 * i)
                        turn_x(e + 1, 2 * i + 1)

            run(pe, lambda: [turn_x(0, i) for i in range(4)], turn)

        @block.scalar
        def _(act):
            def hi_w1(e, k):
                act.wait_ge(w1_loaded, e * 16 + 16)
                wait(act, up_done, e * CH)
                act.activation(w1_hi[:, k, :], w1_raw[:, k, :], ACT.Copy).then_inc(w1_hi_ready, 1)

            def hi_w2(e, k):
                act.wait_ge(w2_loaded, e * 16 + 16)
                wait(act, down_done, e * 4)
                act.activation(w2_hi[:, 4 * k:4 * k + 4, :], w2_raw[:, 4 * k:4 * k + 4, :], ACT.Copy).then_inc(w2_hi_ready, 1)

            def hi_x(e, i):
                half, k = i // 2, i % 2
                act.wait_ge(xe_turned, e * 4 + i + 1)
                wait(act, up_done, e * CH)
                act.activation(xe_hi[:, k, half * HALF:(half + 1) * HALF], x_ps[i % 2][:, 0:HALF], ACT.Copy).then_inc(xe_hi_ready, 1)

            def bias(e, p):
                col = b1_cols[:, e, :] if isinstance(e, int) else b1_cols[:, bass.ds(e, 1), :].rearrange("p a c -> p (a c)")
                act.activation(b1_col[p][:, :], col, ACT.Copy).then_inc(b1_ready, 1)

            def gelu(e, p, i):
                if i == 0:
                    act.wait_ge(b1_ready, e + 1)
                act.wait_ge(up_done, e * CH + i + 1)
                wait(act, he_ready, e * CH + i - 3)
                act.activation(act_out[i % 4][:, :], u_ps[i % 4][:, 0:HALF], ACT.Gelu,
                               bias=b1_col[p][:, i % FCH:i % FCH + 1]).then_inc(gelu_done, 1)

            def weigh(e, p, i):
                act.wait_ge(y_biased, e * 4 + i + 1)
                if i == 0:
                    wait(act, scattered, e * (16 * TJ))
                for j in range(2):
                    last = act.activation(y_sb[:, 2 * i + j, :], y_bias[i % 2][:, j, :], ACT.Copy,
                                          scale=weight[p][:, 2 * i + j:2 * i + j + 1])
                last.then_inc(y_ready, 1)

            def first():
                for k in range(2):
                    hi_w1(0, k)
                for i in range(4):
                    hi_x(0, i)
                bias(0, 0)

            def turn(e, p, more):
                for i in range(CH):
                    gelu(e, p, i)
                    if i in (1, 5):
                        hi_w2(e, i // 4)
                if more:
                    bias(e + 1, 1 - p)
                    hi_w1(e + 1, 0)
                    hi_x(e + 1, 0)
                    hi_x(e + 1, 1)
                weigh(e, p, 0)
                if more:
                    hi_w1(e + 1, 1)
                    hi_x(e + 1, 2)
                    hi_x(e + 1, 3)
                for i in range(1, 4):
                    weigh(e, p, i)

            run(act, first, turn)

        @block.vector
        def _(dve):
            def lo_w1(e, k):
                dve.wait_ge(w1_hi_ready, e * 2 + k + 1)
                dve.tensor_tensor(w1_lo[:, k, :], w1_raw[:, k, :], w1_hi[:, k, :].bitcast(F32), ALU.subtract).then_inc(w1_ready, 1)

            def lo_w2(e, k):
                c = slice(4 * k, 4 * k + 4)
                dve.wait_ge(w2_hi_ready, e * 2 + k + 1)
                dve.tensor_tensor(w2_lo[:, c, :], w2_raw[:, c, :], w2_hi[:, c, :].bitcast(F32), ALU.subtract).then_inc(w2_ready, 1)

            def lo_x(e, i):
                half, k = i // 2, i % 2
                cols = slice(half * HALF, (half + 1) * HALF)
                dve.wait_ge(xe_hi_ready, e * 4 + i + 1)
                dve.tensor_tensor(xe_lo[:, k, cols], x_ps[i % 2][:, 0:HALF], xe_hi[:, k, cols].bitcast(F32),
                                  ALU.subtract).then_inc(xe_ready, 1)

            def index(e, p):
                dve.wait_ge(table_loaded, e * 16 + 16)
                wait(dve, gathered, e * (16 * TJ))
                dve.tensor_copy(token[:, :], entries[:, :, 0]).then_inc(index_step, 1)
                dve.wait_ge(index_step, e + 1)
                dve.tensor_scalar(source[:, :], token[:, :], float(ROWS - 1), None, ALU.min)
                wait(dve, scattered, (e - 1) * (16 * TJ))
                dve.tensor_tensor(target[p][:, :], token[:, :], spare[:, :], ALU.min)
                dve.tensor_copy(weight[p][:, :], entries[:, :, 1].bitcast(F32)).then_inc(source_ready, 1)

            def split(e, i):
                half, c = i // FCH, i % FCH
                if c == 0:
                    wait(dve, down_done, e * 4 - 2 + 2 * half)
                dve.wait_ge(gelu_done, e * CH + i + 1)
                dve.tensor_copy(he_hi[:, half, c, :], act_out[i % 4][:, :]).then_inc(he_hi_done, 1)
                dve.wait_ge(he_hi_done, e * CH + i + 1)
                dve.tensor_tensor(he_lo[:, half, c, :], act_out[i % 4][:, :], he_hi[:, half, c, :].bitcast(F32),
                                  ALU.subtract).then_inc(he_ready, 1)

            def bias(e, i):
                if i == 0:
                    dve.wait_ge(b2_loaded, e * 16 + 16)
                wait(dve, y_ready, e * 4 + i - 1)
                dve.wait_ge(down_done, e * 4 + i + 1)
                dve.tensor_tensor(y_bias[i % 2][:, :, :], y_ps[i % 2][:, :, :],
                                  b2_row[:, :].unsqueeze(1).to_broadcast([SP, 2, D]), ALU.add).then_inc(y_biased, 1)

            def first():
                dve.wait_ge(spare_ready, 1)
                index(0, 0)
                for k in range(2):
                    lo_w1(0, k)
                for i in range(4):
                    lo_x(0, i)

            def turn(e, p, more):
                for i in range(CH):
                    split(e, i)
                    if i in (1, 5):
                        lo_w2(e, i // 4)
                    if i == 3 and more:
                        index(e + 1, 1 - p)
                bias(e, 0)
                if more:
                    lo_w1(e + 1, 0)
                    lo_x(e + 1, 0)
                    lo_x(e + 1, 1)
                bias(e, 1)
                if more:
                    lo_w1(e + 1, 1)
                    lo_x(e + 1, 2)
                    lo_x(e + 1, 3)
                bias(e, 2)
                bias(e, 3)

            run(dve, first, turn)


def finish(nc, sum_rows, out):
    PARTS = 4
    with ExitStack() as ctx:
        copied = ctx.enter_context(nc.semaphore("copied"))
        block = ctx.enter_context(nc.Block())
        out_f = out.rearrange("i n d -> (i n) d")

        @block.sync
        def _(sp):
            for i in range(PARTS):
                r = slice(ROWS // PARTS * i, ROWS // PARTS * (i + 1))
                sp.dma_start(out_f[r, :], sum_rows[r, :]).then_inc(copied, 16)
            sp.wait_ge(copied, 16 * PARTS)


_INS = ['x', 'cls_tok', 'L0_tok_W_embed', 'L0_tok_b_embed', 'L0_tok_pos_embed', 'L0_attn_W_qkv', 'L0_attn_b_qkv',
        'L0_attn_W_proj', 'L0_attn_b_proj', 'L0_attn_proj_mat', 'L0_ffn_gate_w', 'L0_ffn_gate_b', 'L0_ffn_w1',
        'L0_ffn_b1', 'L0_ffn_w2', 'L0_ffn_b2']
_OUTS = [((IMAGES, TOKENS, D), 'float32')]


def kernel(**inputs):
    import numpy as _np
    import concourse.bacc as _bacc
    from concourse import mybir as _mybir
    from concourse.bass_utils import run_bass_kernel_spmd as _run

    nc = _bacc.Bacc("TRN2", target_bir_lowering=False, num_devices=1)
    arrays, args = {}, []
    for name in _INS:
        a = _np.ascontiguousarray(inputs[name])
        arrays[f"in_{name}_dram"] = a
        args.append(nc.dram_tensor(f"in_{name}_dram", a.shape, _mybir.dt.from_np(a.dtype), kind="ExternalInput").ap())
    for i, (shape, dtype) in enumerate(_OUTS):
        dt = _mybir.dt.from_np(_np.dtype(dtype))
        args.append(nc.dram_tensor(f"out_{i}_dram", shape, dt, kind="ExternalOutput").ap())
    tower_kernel(nc, *args)
    r = _run(nc, [arrays], core_ids=[0])
    got = tuple(r.results[0][f"out_{i}_dram"] for i in range(len(_OUTS)))
    return got[0]
```

```python
from contextlib import ExitStack

import concourse.bass as bass
from concourse import mybir

F32 = mybir.dt.float32
F32R = mybir.dt.float32r
BF16 = mybir.dt.bfloat16
U32 = mybir.dt.uint32
ALU = mybir.AluOpType
ACT = mybir.ActivationFunctionType
AX_X = mybir.AxisListType.X

IMAGES, CHANNELS, SIDE, PATCH = 64, 3, 224, 16
GRID = SIDE // PATCH
PATCHES = GRID * GRID
TOKENS = PATCHES + 1
ROWS = IMAGES * TOKENS
D = 256
HEADS, HEAD, FEATS = 16, 16, 64
KCH = D // 128
PCH = CHANNELS * PATCH * PATCH // 128
GROUP = 8
GP = GROUP * GRID
TA = (TOKENS + 1) // 2
TB = TOKENS - TA
T2 = 2 * TA
PAIRS = HEADS // 2
BR = 33
KVW = 2 * HEAD + 2
KV_MOVED = 512 // PAIRS
O_PAIRS = 3
EXPERTS, TOPK, HIDDEN = 32, 2, 1024
CAP = -(-int(ROWS * TOPK * 12) // (EXPERTS * 10))
TJ = 8
EMPTY_PARTS = 7
SP = -(-CAP // TJ)
SLOTS = SP * TJ
EMPTY_SLOTS = EXPERTS * SLOTS // (128 * EMPTY_PARTS)
HALF = SLOTS // 2
FCH = HIDDEN // 128
ENTRY = 16
OUTSIDE = 65536.0
EPS = 1e-5
FEAT_EPS = 1e-4
DEN_EPS = 1e-6


class At:

    def __init__(self, base, c):
        self.known = c if base is None else None
        self.n = c if base is None else base * 2 + c
        self.half = c // 2 if base is None else base + c // 2
        self.par = c % 2


def inside(at):
    return at.known is None or 0 <= at.known < IMAGES


def wait(eng, sem, value, carrier=None):
    if isinstance(value, int):
        if value > 0:
            eng.wait_ge(sem, value)
        return
    eng.wait_ge(sem, value)
    if carrier is not None:
        eng.sem_inc(carrier, 1)


def upto(at, ahead=0, per=1, part=None):
    part = per if part is None else part
    if at.known is None:
        return (at.n + ahead) * per + part
    return min((at.known + ahead) * per + part, IMAGES * per)


def linker(eng, sem, base, carrier=None):
    count = [0]

    def link(ins):
        count[0] += 1
        ins.then_inc(sem, 1)
        wait(eng, sem, base + count[0], carrier)
    return link


def three(pe, out, w_hi, w_lo, x_hi, x_lo, start, stop):
    pe.matmul(out, w_hi, x_hi, start=start, stop=False)
    pe.matmul(out, w_hi, x_lo, start=False, stop=False)
    return pe.matmul(out, w_lo, x_hi, start=False, stop=stop)


def tower_kernel(nc, x, cls_tok, w_embed, b_embed, pos_embed, w_qkv, b_qkv, w_proj, b_proj,
                 proj_mat, gate_w, gate_b, w1, b1, w2, b2, out):
    h_rows = nc.dram_tensor("h_rows", [(IMAGES + 1) * TOKENS, D], F32, kind="Internal").ap()
    sum_rows = nc.dram_tensor("sum_rows", [ROWS + SLOTS, D], F32, kind="Internal").ap()
    x2_rows = nc.dram_tensor("x2_rows", [ROWS, D], F32, kind="Internal").ap()
    slot_table = nc.dram_tensor("slot_table", [EXPERTS * SLOTS, ENTRY], U32, kind="Internal").ap()

    with ExitStack() as ctx:
        def sb(name, shape, dt):
            return ctx.enter_context(nc.sbuf_tensor(name, shape, dt))

        ident = sb("ident", [128, 128], F32)
        b1_cols = sb("b1_cols", [128, EXPERTS, FCH], F32)
        keep = dict(ident=ident, b1_cols=b1_cols)
        with ExitStack() as attn_ctx:
            def ab(name, shape, dt):
                return attn_ctx.enter_context(nc.sbuf_tensor(name, shape, dt))

            keep.update(
                wqkv_hi=ab("wqkv_hi", [128, KCH, 3 * D], F32R), wqkv_lo=ab("wqkv_lo", [128, KCH, 3 * D], F32R),
                wp_hi=ab("wp_hi", [128, KCH, D], F32R), wp_lo=ab("wp_lo", [128, KCH, D], F32R),
                pb_hi=ab("pb_hi", [128, 512], F32R), pb_lo=ab("pb_lo", [128, 512], F32R),
                bqk=ab("bqk", [128, 4], F32), bv=ab("bv", [BR, D], F32R), one_rows=ab("one_rows", [BR, TA], F32R), bp=ab("bp", [128, D], F32),
                gw=ab("gw", [128, KCH, EXPERTS], F32), gb=ab("gb", [128, 2, EXPERTS], F32),
                before=ab("before", [TA, TA], BF16), ones=ab("ones", [TA, TA], BF16),
                kv_mask=ab("kv_mask", [128, KVW], F32), expert_no=ab("expert_no", [128, EXPERTS], F32),
                feat_eps=ab("feat_eps", [128, 1], F32), ln_eps=ab("ln_eps", [128, 1], F32))
            with ExitStack() as embed_ctx:
                early = dict(
                    empty=embed_ctx.enter_context(nc.sbuf_tensor("empty", [128, EMPTY_SLOTS, ENTRY], U32)),
                    zero_rows=embed_ctx.enter_context(nc.sbuf_tensor("zero_rows", [SP, 2, D], F32)),
                    raw0=embed_ctx.enter_context(nc.sbuf_tensor("raw0", [GP, CHANNELS, PATCH * SIDE], F32)),
                    we_raw=embed_ctx.enter_context(nc.sbuf_tensor("we_raw", [128, PCH, D], F32)),
                    raw0_loaded=embed_ctx.enter_context(nc.semaphore("raw_loaded0")),
                    we_loaded=embed_ctx.enter_context(nc.semaphore("we_loaded")))
                prepare(nc, keep, early, x, w_embed, w_qkv, b_qkv, w_proj, b_proj, proj_mat, gate_w, gate_b, b1,
                        cls_tok, h_rows)
                embed(nc, keep, early, x, b_embed, pos_embed, h_rows, slot_table, sum_rows)
            attend(nc, keep, h_rows, sum_rows, x2_rows, slot_table)
        experts(nc, keep, w1, w2, b2, x2_rows, sum_rows, slot_table)
        finish(nc, sum_rows, out)


def images_in(x, g, b):
    n = g * GROUP + b
    image = x[n:n + 1, :, :, :] if isinstance(n, int) else x[bass.ds(n, 1), :, :, :]
    return image.rearrange("a c (ph py) w -> (a ph) c (py w)", py=PATCH)


def prepare(nc, keep, early, x, w_embed, w_qkv, b_qkv, w_proj, b_proj, proj_mat, gate_w, gate_b, b1,
            cls_tok, h_rows):
    ident, b1_cols = keep["ident"], keep["b1_cols"]
    QCH = 3 * D // 128
    with ExitStack() as ctx:
        def sb(name, shape, dt):
            return ctx.enter_context(nc.sbuf_tensor(name, shape, dt))

        def sem(name):
            return ctx.enter_context(nc.semaphore(name))

        wqkv_raw = sb("wqkv_raw", [128, QCH, D], F32)
        wp_raw = sb("wp_raw", [128, KCH, D], F32)
        pb_raw = sb("pb_raw", [128, 512], F32)
        bv_raw, bv_hi = sb("bv_raw", [BR, D], F32), sb("bv_hi", [BR, D], F32R)
        b1_raw = sb("b1_raw", [EXPERTS, HIDDEN], F32)
        cls_sb = sb("cls_sb", [IMAGES + 1, D], F32)
        empty_f = sb("empty_f", [128, ENTRY], F32)
        empty, zero_rows = early["empty"], early["zero_rows"]
        ps = [ctx.enter_context(nc.psum_tensor(f"prep_ps{i}", [128, 512], F32)) for i in range(5)]
        w_loaded, pb_zeroed, pb_loaded, cls_loaded, stored = (
            sem("w_loaded"), sem("pb_zeroed"), sem("pb_loaded"), sem("cls_loaded"), sem("prep_stored"))
        ident_zeroed, ident_ready, small = sem("ident_zeroed"), sem("ident_ready"), sem("small_step")
        turned, hi_ready, lo_ready, empty_ready, pool_step = (
            sem("turned"), sem("prep_hi"), sem("prep_lo"), sem("empty_ready"), sem("prep_pool_step"))
        block = ctx.enter_context(nc.Block())

        @block.sync
        def _(sp):
            sp.dma_start(wqkv_raw[:, :, :], w_qkv.rearrange("(m p) k -> p m k", p=128)).then_inc(w_loaded, 16)
            sp.dma_start(wp_raw[:, :, :], w_proj.rearrange("(m p) k -> p m k", p=128)).then_inc(w_loaded, 16)
            sp.dma_start(b1_raw[:, :], b1).then_inc(w_loaded, 16)
            sp.dma_start(keep["gw"][:, :, :], gate_w.rearrange("(k p) e -> p k e", p=128)).then_inc(w_loaded, 16)
            sp.dma_start(keep["bp"][:, :], b_proj.partition_broadcast(128)).then_inc(w_loaded, 16)
            for t in range(2):
                sp.dma_start(keep["gb"][:, t, :], gate_b.partition_broadcast(128)).then_inc(w_loaded, 16)
            with nc.allow_non_contiguous_dma(reason="512 biases, one a partition"):
                sp.dma_start(keep["bqk"][:, :], b_qkv[0:512].rearrange("(m p) -> p m", p=128)).then_inc(w_loaded, 16)
            sp.dma_start(cls_sb[:, :], cls_tok[0, 0, :].partition_broadcast(IMAGES + 1)).then_inc(cls_loaded, 16)
            sp.wait_ge(pb_zeroed, 2)
            for r in (0, BR - 1):
                sp.dma_start(bv_raw[r:r + 1, :], b_qkv[2 * D:3 * D].partition_broadcast(1)).then_inc(pb_loaded, 16)
            with nc.allow_non_contiguous_dma(reason="64 x 16 projection, transposed, once a head"):
                for h in range(128 // HEAD):
                    sp.dma_start(pb_raw[h * HEAD:(h + 1) * HEAD, h * FEATS:(h + 1) * FEATS],
                                 proj_mat.rearrange("f d -> d f")).then_inc(pb_loaded, 16)
            sp.wait_ge(cls_loaded, 16)
            sp.dma_start(h_rows.rearrange("(i n) d -> i n d", n=TOKENS)[:, 0, :], cls_sb[:, :]).then_inc(stored, 16)
            sp.wait_ge(stored, 16)

        @block.gpsimd
        def _(pool):
            link = linker(pool, pool_step, 0)
            pool.memset(pb_raw[:, :], 0.0).then_inc(pb_zeroed, 1)
            pool.memset(bv_raw[:, :], 0.0).then_inc(pb_zeroed, 1)
            pool.memset(ident[:, :], 0.0).then_inc(ident_zeroed, 1)
            pool.wait_ge(ident_zeroed, 1)
            pool.affine_select(out=ident[:, :], in_=ident[:, :], compare_op=ALU.not_equal, fill=1.0,
                               base=0, pattern=[[-1, 128]], channel_multiplier=1).then_inc(ident_ready, 1)
            pool.iota(keep["expert_no"][:, :], pattern=[[1, EXPERTS]], base=0, channel_multiplier=0,
                      allow_small_or_imprecise_dtypes=True).then_inc(small, 1)
            link(pool.memset(keep["ones"][:, :], 1.0))
            pool.affine_select(out=keep["before"][:, :], in_=keep["ones"][:, :], compare_op=ALU.is_gt, fill=0.0,
                               base=0, pattern=[[1, TA]], channel_multiplier=-1).then_inc(small, 1)
            pool.memset(keep["feat_eps"][:, :], FEAT_EPS).then_inc(small, 1)
            pool.memset(keep["ln_eps"][:, :], EPS).then_inc(small, 1)
            pool.memset(zero_rows[:, :, :], 0.0).then_inc(small, 1)
            link(pool.memset(keep["kv_mask"][:, :], 0.0))
            for p0, c0, c1 in ((0, 0, HEAD), (0, 2 * HEAD, 2 * HEAD + 1), (64, HEAD, 2 * HEAD), (64, 2 * HEAD + 1, KVW)):
                pool.memset(keep["kv_mask"][p0:p0 + 64, c0:c1], 1.0).then_inc(small, 1)
            pool.wait_ge(small, 9)

        @block.tensor
        def _(pe):
            pe.wait_ge(ident_ready, 1)
            pe.wait_ge(w_loaded, 16 * 8)
            for k in range(KCH):
                for m in range(QCH):
                    n = k * QCH + m
                    pe.transpose(ps[n // 4][:, n % 4 * 128:n % 4 * 128 + 128],
                                 wqkv_raw[:, m, k * 128:(k + 1) * 128], ident[:, :])
            for k in range(KCH):
                for m in range(KCH):
                    n = k * KCH + m
                    last = pe.transpose(ps[3][:, n * 128:n * 128 + 128],
                                        wp_raw[:, m, k * 128:(k + 1) * 128], ident[:, :])
            for c in range(FCH):
                last = pe.transpose(ps[4][:, c * EXPERTS:(c + 1) * EXPERTS], b1_raw[:, c * 128:(c + 1) * 128],
                                    ident[0:EXPERTS, 0:EXPERTS])
            last.then_inc(turned, 1)

        @block.scalar
        def _(act):
            for b in range(GROUP):
                act.dma_start(early["raw0"][b * GRID:(b + 1) * GRID, :, :], images_in(x, 0, b)).then_inc(early["raw0_loaded"], 16)
            act.dma_start(early["we_raw"][:, :, :], w_embed.rearrange("(j p) e -> p j e", p=128)).then_inc(early["we_loaded"], 16)
            act.wait_ge(turned, 1)
            for i in range(3):
                act.activation(keep["wqkv_hi"][:, :, :].rearrange("p k m -> p (k m)")[:, i * 512:(i + 1) * 512],
                               ps[i][:, :], ACT.Copy).then_inc(hi_ready, 1)
            act.activation(keep["wp_hi"][:, :, :].rearrange("p k m -> p (k m)"), ps[3][:, :], ACT.Copy).then_inc(hi_ready, 1)
            act.activation(b1_cols[:, :, :], ps[4][:, 0:FCH * EXPERTS].rearrange("p (c e) -> p e c", e=EXPERTS),
                           ACT.Copy).then_inc(hi_ready, 1)
            act.wait_ge(pb_loaded, 16 * 10)
            act.activation(bv_hi[:, :], bv_raw[:, :], ACT.Copy).then_inc(hi_ready, 1)
            act.activation(keep["pb_hi"][:, :], pb_raw[:, :], ACT.Copy, scale=float(HEAD) ** -0.25).then_inc(hi_ready, 1)
            act.wait_ge(hi_ready, 7)

        @block.vector
        def _(dve):
            dve.memset(empty_f[:, :], 0.0).then_inc(lo_ready, 1)
            dve.wait_ge(lo_ready, 1)
            dve.memset(empty_f[:, 0:1], float(ROWS + SLOTS)).then_inc(lo_ready, 1)
            dve.wait_ge(lo_ready, 2)
            dve.tensor_copy(empty[:, :, :], empty_f[:, :].unsqueeze(1).to_broadcast([128, EMPTY_SLOTS, ENTRY])).then_inc(empty_ready, 1)
            dve.wait_ge(empty_ready, 1)
            for i in range(4):
                dve.wait_ge(hi_ready, i + 1)
                hi = keep["wqkv_hi"] if i < 3 else keep["wp_hi"]
                lo = keep["wqkv_lo"] if i < 3 else keep["wp_lo"]
                at = slice(i % 3 * 512, i % 3 * 512 + 512)
                dve.tensor_tensor(lo[:, :, :].rearrange("p k m -> p (k m)")[:, at], ps[i][:, :],
                                  hi[:, :, :].bitcast(F32).rearrange("p k m -> p (k m)")[:, at],
                                  ALU.subtract).then_inc(lo_ready, 1)
            dve.wait_ge(hi_ready, 7)
            dve.scalar_tensor_tensor(keep["pb_lo"][:, :], pb_raw[:, :], float(HEAD) ** -0.25,
                                     keep["pb_hi"][:, :].bitcast(F32), ALU.mult, ALU.subtract).then_inc(lo_ready, 1)
            dve.tensor_copy(keep["bv"][0:BR - 1, :], bv_hi[0:BR - 1, :].bitcast(F32))
            dve.tensor_tensor(keep["bv"][BR - 1:BR, :], bv_raw[BR - 1:BR, :], bv_hi[BR - 1:BR, :].bitcast(F32), ALU.subtract)
            dve.memset(keep["one_rows"][:, :].bitcast(F32), 1.0).then_inc(lo_ready, 1)
            dve.wait_ge(lo_ready, 8)


def embed(nc, keep, early, x, b_embed, pos_embed, h_rows, slot_table, sum_rows):
    ident = keep["ident"]
    GROUPS = IMAGES // GROUP
    with ExitStack() as ctx:
        def sb(name, shape, dt):
            return ctx.enter_context(nc.sbuf_tensor(name, shape, dt))

        def sem(name):
            return ctx.enter_context(nc.semaphore(name))

        we_raw, w_loaded = early["we_raw"], early["we_loaded"]
        we_hi, we_lo = sb("we_hi", [128, PCH, D], F32R), sb("we_lo", [128, PCH, D], F32R)
        pos_b = sb("pos_b", [GP, GRID, D], F32)
        be = sb("be", [GP, D], F32)
        raw = [early["raw0"], sb("raw1", [GP, CHANNELS, PATCH * SIDE], F32)]
        patch = [sb(f"patch{r}", [GP, PCH * 128], F32) for r in range(2)]
        xt_hi = [sb(f"xt_hi{r}", [128, PCH, GP], F32R) for r in range(2)]
        xt_lo = [sb(f"xt_lo{r}", [128, PCH, GP], F32R) for r in range(2)]
        h_out = [sb(f"h_out{p}", [GP, GRID, D], F32) for p in range(2)]
        xt_ps = [ctx.enter_context(nc.psum_tensor(f"xt_ps{r}", [128, 2, 512], F32)) for r in range(2)]
        h_ps = [ctx.enter_context(nc.psum_tensor(f"h_ps{r}", [GP, 512], F32)) for r in range(2)]
        w_hi, w_ready, pos_loaded, pos_ready = sem("we_hi_done"), sem("we_ready"), sem("pos_loaded"), sem("pos_ready")
        raw_loaded = [early["raw0_loaded"], sem("raw_loaded1")]
        filled = sem("filled")
        regrouped, regrouped_dve = sem("regrouped"), sem("regrouped_dve")
        turned, hi_ready, lo_ready, h_summed, h_added, h_stored = (
            sem("xt_turned"), sem("xt_hi_ready"), sem("xt_lo_ready"), sem("h_summed"), sem("h_added"), [sem(f"h_stored{p}") for p in range(2)])
        waited = sem("waited")
        block = ctx.enter_context(nc.Block())
        UNITS = GRID
        BY_DVE = (6, 13)
        N_DVE, N_POOL = len(BY_DVE), UNITS - len(BY_DVE)

        def regroup(eng, p, w):
            return eng.tensor_copy(patch[w % 2][:, :].rearrange("p (r x) -> p r x", x=PATCH),
                                   raw[p][:, :, :].rearrange("p c (y x) -> p (c y) x", x=SIDE)[:, :, w * PATCH:(w + 1) * PATCH])

        def xt3(t):
            return t[:, :, :].rearrange("p (a b) t -> p a (b t)", a=2)

        @block.sync
        def _(sp):
            def load(g, p):
                for b in range(GROUP):
                    sp.dma_start(raw[p][b * GRID:(b + 1) * GRID, :, :], images_in(x, g, b)).then_inc(raw_loaded[p], 16)

            sp.dma_start(be[:, :], b_embed.partition_broadcast(GP)).then_inc(pos_loaded, 16)
            for b in range(GROUP):
                sp.dma_start(pos_b[b * GRID:(b + 1) * GRID, :, :],
                             pos_embed[0].rearrange("(ph pw) e -> ph pw e", pw=GRID)).then_inc(pos_loaded, 16)
            load(1, 1)
            for q in range(EMPTY_PARTS):
                sp.dma_start(slot_table.rearrange("(q p s) w -> q p s w", q=EMPTY_PARTS, p=128)[q], early["empty"][:, :, :])                    .then_inc(filled, 16)
            for j in range(0, TJ, 2):
                sp.dma_start(sum_rows[ROWS:ROWS + SLOTS, :].rearrange("(p j) d -> p j d", j=TJ)[:, j:j + 2, :],
                             early["zero_rows"][:, :, :]).then_inc(filled, 16)

            def store(g, p):
                wait(sp, h_added, g * UNITS + UNITS, waited)
                for b in range(GROUP):
                    row = (g * GROUP + b) * TOKENS + 1
                    dst = h_rows[bass.ds(row, PATCHES), :] if not isinstance(row, int) else h_rows[row:row + PATCHES, :]
                    sp.dma_start(dst.rearrange("(ph pw) e -> ph pw e", pw=GRID),
                                 h_out[p][b * GRID:(b + 1) * GRID, :, :]).then_inc(h_stored[p], 16)

            with sp.Fori(1, GROUPS // 2) as it:
                for p in range(2):
                    wait(sp, regrouped, it * (2 * N_POOL) + (p - 1) * N_POOL, waited)
                    wait(sp, regrouped_dve, it * (2 * N_DVE) + (p - 1) * N_DVE, waited)
                    load(it * 2 + p, p)
                    store(it * 2 + (p - 2), p)
            for p in range(2):
                store(GROUPS - 2 + p, p)
            for p in range(2):
                wait(sp, h_stored[p], 16 * GROUP * GROUPS // 2, waited)
            wait(sp, filled, 16 * (EMPTY_PARTS + TJ // 2))

        @block.gpsimd
        def _(pool):
            def group(g, half, p):
                wait(pool, raw_loaded[p], half * (16 * GROUP) + 16 * GROUP, waited)
                for w in range(GRID):
                    if w not in BY_DVE:
                        wait(pool, turned, g * UNITS + w - 1, waited)
                        regroup(pool, p, w).then_inc(regrouped, 1)

            for p in range(2):
                group(p, 0, p)
            with pool.Fori(1, GROUPS // 2) as it:
                for p in range(2):
                    group(it * 2 + p, it, p)

        @block.tensor
        def _(pe):
            def turn(g, n, w):
                if w in BY_DVE:
                    pe.wait_ge(regrouped_dve, g * N_DVE + BY_DVE.index(w) + 1)
                else:
                    pe.wait_ge(regrouped, g * N_POOL + w - sum(u < w for u in BY_DVE) + 1)
                wait(pe, lo_ready, n - 1)
                for j in range(PCH):
                    last = pe.transpose(xt_ps[w % 2][:, j // 3, j % 3 * GP:(j % 3 + 1) * GP],
                                        patch[w % 2][:, j * 128:(j + 1) * 128], ident[0:GP, 0:GP])
                last.then_inc(turned, 1)

            def product(n, w):
                pe.wait_ge(lo_ready, n + 1)
                wait(pe, h_added, n - 1)
                for j in range(PCH):
                    last = three(pe, h_ps[w % 2][:, 0:D], xt_hi[w % 2][:, j, :], xt_lo[w % 2][:, j, :],
                                 we_hi[:, j, :], we_lo[:, j, :], j == 0, j == PCH - 1)
                last.then_inc(h_summed, 1)

            def group(g, start=0):
                base = g * UNITS
                for w in range(start, GRID + 1):
                    if w < GRID:
                        turn(g, base + w, w)
                    if w > 0:
                        product(base + w - 1, w - 1)

            turn(0, 0, 0)
            pe.wait_ge(w_ready, 1)
            group(0, 1)
            with pe.Fori(1, GROUPS) as g:
                group(g)

        @block.scalar
        def _(act):
            act.wait_ge(w_loaded, 16)
            act.activation(we_hi[:, :, :], we_raw[:, :, :], ACT.Copy).then_inc(w_hi, 1)

            def group(g):
                for w in range(GRID):
                    n = g * UNITS + w
                    act.wait_ge(turned, n + 1)
                    wait(act, h_summed, n - 1)
                    act.activation(xt3(xt_hi[w % 2]), xt_ps[w % 2][:, :, 0:3 * GP], ACT.Copy).then_inc(hi_ready, 1)

            group(0)
            with act.Fori(1, GROUPS) as g:
                group(g)

        @block.vector
        def _(dve):
            dve.wait_ge(w_hi, 1)
            dve.tensor_tensor(we_lo[:, :, :], we_raw[:, :, :], we_hi[:, :, :].bitcast(F32), ALU.subtract).then_inc(w_ready, 1)
            dve.wait_ge(pos_loaded, 16 * (1 + GROUP))
            dve.tensor_tensor(pos_b[:, :, :], pos_b[:, :, :], be[:, :].unsqueeze(1).to_broadcast([GP, GRID, D]),
                              ALU.add).then_inc(pos_ready, 1)
            dve.wait_ge(pos_ready, 1)

            def low(n, w):
                dve.wait_ge(hi_ready, n + 1)
                dve.tensor_tensor(xt3(xt_lo[w % 2]), xt_ps[w % 2][:, :, 0:3 * GP], xt3(xt_hi[w % 2]).bitcast(F32),
                                  ALU.subtract).then_inc(lo_ready, 1)

            def add(n, p, w):
                dve.wait_ge(h_summed, n + 1)
                dve.tensor_tensor(h_out[p][:, w, :], h_ps[w % 2][:, 0:D], pos_b[:, w, :], ALU.add).then_inc(h_added, 1)

            def group(g, half, p):
                base = g * UNITS
                for w in range(GRID + 1):
                    if w + 1 in BY_DVE:
                        if w + 1 == BY_DVE[0]:
                            wait(dve, raw_loaded[p], half * (16 * GROUP) + 16 * GROUP)
                        wait(dve, turned, base + w)
                        regroup(dve, p, w + 1).then_inc(regrouped_dve, 1)
                    if w < GRID:
                        low(base + w, w)
                    if w == 1:
                        wait(dve, h_stored[p], half * (16 * GROUP))
                    if w > 0:
                        add(base + w - 1, p, w - 1)

            for p in range(2):
                group(p, 0, p)
            with dve.Fori(1, GROUPS // 2) as it:
                for p in range(2):
                    group(it * 2 + p, it, p)


def attend(nc, keep, h_rows, sum_rows, x2_rows, slot_table):
    ident = keep["ident"]
    wqkv_hi, wqkv_lo, wp_hi, wp_lo = keep["wqkv_hi"], keep["wqkv_lo"], keep["wp_hi"], keep["wp_lo"]
    pb_hi, pb_lo, bqk, bv, bp, gw, gb = (keep[k] for k in ("pb_hi", "pb_lo", "bqk", "bv", "bp", "gw", "gb"))
    before, ones, kv_mask, expert_no = keep["before"], keep["ones"], keep["kv_mask"], keep["expert_no"]
    feat_eps, ln_eps, one_rows = keep["feat_eps"], keep["ln_eps"], keep["one_rows"]
    with ExitStack() as ctx:
        def sb(name, shape, dt=F32):
            return ctx.enter_context(nc.sbuf_tensor(name, shape, dt))

        def two(name, shape, dt=F32):
            return [sb(f"{name}{p}", shape, dt) for p in range(2)]

        def sem(name):
            return ctx.enter_context(nc.semaphore(name))

        h_in, res = two("h_in", [TA, 2, D]), two("res", [TA, 2, D])
        xn, x2 = two("xn", [TA, 2, D]), two("x2", [TA, 2, D])
        mv1, mv2 = two("mv1_", [TA, 2, 2]), two("mv2_", [TA, 2, 2])
        lnv1, lnv2 = two("lnv1_", [TA, 2]), two("lnv2_", [TA, 2])
        y01, y02 = two("y01_", [TA, 2]), two("y02_", [TA, 2])
        scale1, scale2 = two("scale1_", [TA, 2]), two("scale2_", [TA, 2])
        shift1, shift2 = two("shift1_", [TA, 2]), two("shift2_", [TA, 2])
        hot, hot_sum, top_no = two("hot", [TA, 4, EXPERTS]), two("hot_sum", [TA, 2, EXPERTS], BF16), two("top_no", [TA, 2, 2])
        seen = two("seen", [TA, EXPERTS], BF16)
        gap, e_gap, rec_w = two("gap", [TA, 2]), two("e_gap", [TA, 2]), two("rec_w", [TA, 2])
        pos4, slot, entry = two("pos4_", [TA, 4]), two("slot", [TA, 4], U32), two("entry", [TA, 4, ENTRY], U32)
        fmax, den, rec = two("fmax", [TA, HEADS]), two("den", [TA, PAIRS, 2]), two("rec", [TA, PAIRS, 2])
        stat1, stat2 = sb("stat1", [TA, 2, 6]), sb("stat2", [TA, 2, 6])
        ln_t1, ln_t2 = ([sb(f"ln_t{n}_{i}", [TA, 2]) for i in range(4)] for n in (1, 2))
        x_hi, x_lo = sb("x_hi", [128, KCH, T2], F32R), sb("x_lo", [128, KCH, T2], F32R)
        qk_hi, qk_lo = sb("qk_hi", [128, 4, T2], F32R), sb("qk_lo", [128, 4, T2], F32R)
        v_flat = sb("v_flat", [TA, 2 * PAIRS * KVW + KV_MOVED - KVW])
        v_ext = v_flat[:, 0:2 * PAIRS * KVW].rearrange("p (t j c) -> p t j c", t=2, j=PAIRS)
        feat = [sb(f"feat{u}", [TA, HEADS, FEATS]) for u in range(4)]
        kvb = sb("kvb", [128, PAIRS + O_PAIRS - 1, KVW])
        qt = [sb(f"qt{j}", [128, 4, TA]) for j in range(4)]
        attn = sb("attn", [TA, 2, D])
        a_hi, a_lo = sb("a_hi", [128, KCH, T2], F32R), sb("a_lo", [128, KCH, T2], F32R)
        x2t = sb("x2t", [128, KCH, T2])
        logit, top_v, top_i = sb("logit", [TA, 2, EXPERTS]), sb("top_v", [TA, 2, 8]), sb("top_i", [TA, 2, 8], U32)
        prod, den_w = sb("prod", [TA, 4, EXPERTS]), sb("den_w", [TA, 2])
        valid, e_w = sb("valid", [TA, 4]), sb("e_w", [TA, 2])
        slot_a, slot_b, slot_c = (sb(f"slot_{c}", [TA, 4]) for c in "abc")
        token_no = sb("token_no", [TA, 4])

        def bank(name, shape):
            return ctx.enter_context(nc.psum_tensor(name, shape, F32))

        f_ps = [bank(f"f_ps{t}", [TA, 2, 512]) for t in range(2)]
        bank_a, bank_b, bank_c, bank_d = (bank(f"bank_{i}", [128, 512]) for i in "abcd")
        gate_ps, pos_ps = (b[:, 0:2 * EXPERTS] for b in (bank_c, bank_a))
        qt_bank = [bank_c, bank_c, bank_d, bank_c]

        h_loaded, res_loaded, h1_stored, x2_stored, slots_stored = (
            [sem(f"{n}{p}") for p in range(2)] for n in ("h_loaded", "res_loaded", "h1_stored", "x2_stored", "slots_stored"))
        set_up, waited = sem("set_up"), sem("waited")
        stat1_done, mv1_ready, lnv1_ready, y01_ready, newton1_step, scale1_ready, xn_ready = (
            sem(n) for n in ("stat1_done", "mv1_ready", "lnv1_ready", "y01_ready", "newton1_step", "scale1_ready", "xn_ready"))
        stat2_done, mv2_ready, lnv2_ready, y02_ready, newton2_step, scale2_ready, x2_ready = (
            sem(n) for n in ("stat2_done", "mv2_ready", "lnv2_ready", "y02_ready", "newton2_step", "scale2_ready", "x2_ready"))
        x_turned, x_hi_ready, x_ready = sem("x_turned"), sem("x_hi_ready"), sem("x_ready")
        k_done, k_hi_ready, k_ready = sem("k_done"), sem("k_hi_ready"), sem("k_ready")
        q_done, q_hi_ready, q_ready = sem("q_done"), sem("q_hi_ready"), sem("q_ready")
        v_done, v_ready = sem("v_done"), sem("v_ready")
        feat_done, feat_maxed, feat_shifted, exp_done = sem("feat_done"), sem("feat_maxed"), sem("feat_shifted"), sem("exp_done")
        kv_done, kvb_ready, q_turned, qt_ready, o_done = sem("kv_done"), sem("kvb_ready"), sem("q_turned"), sem("qt_ready"), sem("o_done")
        den_ready, rec_ready, attn_ready, a_turned, a_hi_ready, a_ready = (
            sem("den_ready"), sem("rec_ready"), sem("attn_ready"), sem("a_turned"), sem("a_hi_ready"), sem("a_ready"))
        proj_done, res_ready, h1_ready, x2_turned, x2t_ready = (
            sem("proj_done"), sem("res_ready"), sem("h1_ready"), sem("x2_turned"), sem("x2t_ready"))
        gate_done, logit_ready, top_v_ready, top_i_ready, top_ready = (
            sem("gate_done"), sem("logit_ready"), sem("top_v_ready"), sem("top_i_ready"), sem("top_ready"))
        hot_ready, hot_sum_ready, seen_step, seen_ready, e_gap_ready = (
            sem("hot_ready"), sem("hot_sum_ready"), sem("seen_step"), sem("seen_ready"), sem("e_gap_ready"))
        pos_done, pos_read, den_w_ready, placed, slot_step, wt_ready = (
            sem("pos_done"), sem("pos_read"), sem("den_w_ready"), sem("placed"), sem("slot_step"), sem("wt_ready"))
        block = ctx.enter_context(nc.Block())

        FIRST, LOOP0, LOOP1, LAST = -2, 6, 62, IMAGES + 4

        def run(eng, pieces):
            def step(base, c):
                for piece, ahead, *args in pieces:
                    at = At(base, c + ahead)
                    if inside(at):
                        piece(at, *args)

            for s in range(FIRST, LOOP0):
                step(None, s)
            with eng.Fori(LOOP0 // 2, LOOP1 // 2) as it:
                for c in range(2):
                    step(it, c)
            for s in range(LOOP1, LAST):
                step(None, s)

        def rows(dram, at, first, count):
            if at.known is None:
                return dram[bass.ds(at.n * TOKENS + first, count), :]
            return dram[at.known * TOKENS + first:at.known * TOKENS + first + count, :]

        def flat(t):
            return t[:, :, :].rearrange("p k t -> p (k t)")

        @block.sync
        def _(sp):
            def load_h(at):
                wait(sp, xn_ready, upto(at, -2), waited)
                sp.dma_start(h_in[at.par][:, :, :], rows(h_rows, at, 0, T2).rearrange("(t p) d -> p t d", t=2))\
                    .then_inc(h_loaded[at.par], 16)

            def load_res(at):
                wait(sp, h1_stored[at.par], at.half * 32, waited)
                wait(sp, x2_ready, upto(at, -2), waited)
                sp.dma_start(res[at.par][:, :, :], rows(h_rows, at, 0, T2).rearrange("(t p) d -> p t d", t=2))\
                    .then_inc(res_loaded[at.par], 16)

            def store_h1(at):
                wait(sp, h1_ready, upto(at), waited)
                for t, n in ((0, TA), (1, TB)):
                    sp.dma_start(rows(sum_rows, at, t * TA, n), res[at.par][0:n, t, :]).then_inc(h1_stored[at.par], 16)

            def store_x2(at):
                wait(sp, x2_ready, upto(at), waited)
                for t, n in ((0, TA), (1, TB)):
                    sp.dma_start(rows(x2_rows, at, t * TA, n), x2[at.par][0:n, t, :]).then_inc(x2_stored[at.par], 16)

            run(sp, [(store_h1, -1), (store_x2, -2), (load_res, 1), (load_h, 2)])
            for p in range(2):
                wait(sp, h1_stored[p], 32 * IMAGES // 2, waited)
                wait(sp, x2_stored[p], 32 * IMAGES // 2, waited)

        @block.gpsimd
        def _(pool):
            pool.iota(token_no[:, :], pattern=[[TA, 2], [0, 2]], base=0, channel_multiplier=1,
                      allow_small_or_imprecise_dtypes=True).then_inc(set_up, 1)
            pool.memset(v_ext[:, :, :, 2 * HEAD:KVW], 1.0)
            pool.memset(v_flat[:, 2 * PAIRS * KVW:], 0.0)
            pool.memset(kvb[:, PAIRS:, :], 0.0).then_inc(set_up, 1)
            pool.memset(seen[0][:, :], 0.0).then_inc(set_up, 1)
            for p in range(2):
                pool.memset(entry[p][:, :, :].bitcast(F32), 0.0).then_inc(set_up, 1)
            wait(pool, set_up, 5)

            def newton(at, y0_ready, mv, y0, temps, scale, shift, step, scale_ready, used):
                link = linker(pool, step, at.n * 4, waited)
                wait(pool, y0_ready, upto(at), waited)
                wait(pool, scale_ready, upto(at, -1), waited)
                wait(pool, used, upto(at, -2), waited)
                t0, t1, t2, minus = (t[:, :] for t in temps)
                y = y0[at.par][:, :]
                pool.tensor_scalar(t0, mv[at.par][:, :, 1], EPS, None, ALU.add)
                pool.tensor_scalar(minus, mv[at.par][:, :, 0], -1.0, None, ALU.mult)
                link(pool.tensor_tensor(t1, y, y, ALU.mult))
                link(pool.tensor_tensor(t2, t1, t0, ALU.mult))
                link(pool.tensor_scalar(t1, t2, -0.5, 1.5, ALU.mult, ALU.add))
                link(pool.tensor_tensor(scale[at.par][:, :], t1, y, ALU.mult))
                pool.tensor_tensor(shift[at.par][:, :], minus, scale[at.par][:, :], ALU.mult).then_inc(scale_ready, 1)

            def newton1(at):
                newton(at, y01_ready, mv1, y01, ln_t1, scale1, shift1, newton1_step, scale1_ready, xn_ready)

            def newton2(at):
                newton(at, y02_ready, mv2, y02, ln_t2, scale2, shift2, newton2_step, scale2_ready, x2_ready)

            def add_bias(at):
                wait(pool, res_loaded[at.par], at.half * 16 + 16, waited)
                pool.tensor_tensor(res[at.par][:, :, :], res[at.par][:, :, :],
                                   bp[0:TA, :].unsqueeze(1).to_broadcast([TA, 2, D]), ALU.add).then_inc(res_ready, 1)

            def slots(at):
                link = linker(pool, slot_step, at.n * 5, waited)
                wait(pool, placed, upto(at), waited)
                wait(pool, wt_ready, upto(at, -1), waited)
                wait(pool, slots_stored[at.par], at.half * 64, waited)
                pool.tensor_scalar(valid[:, :], pos4[at.par][:, :], float(CAP), None, ALU.is_lt)
                link(pool.tensor_scalar(slot_a[:, :], top_no[at.par][:, :, :].rearrange("p t k -> p (t k)"), float(SLOTS), None, ALU.mult))
                pool.tensor_tensor(slot_b[:, :], slot_a[:, :], pos4[at.par][:, :], ALU.add)
                link(pool.tensor_scalar(slot_c[:, :], valid[:, :], -OUTSIDE, OUTSIDE, ALU.mult, ALU.add))
                pool.tensor_copy(entry[at.par][:, :, 0], token_no[:, :])
                link(pool.tensor_tensor(slot_a[:, :], slot_c[:, :], slot_b[:, :], ALU.add))
                pool.tensor_copy(slot[at.par][:, :], slot_a[:, :])
                wait(pool, e_gap_ready, upto(at), waited)
                link(pool.tensor_tensor(e_w[:, :], e_gap[at.par][:, :], rec_w[at.par][:, :], ALU.mult))
                v = valid[:, :].rearrange("p (t k) -> p t k", k=2)
                w = entry[at.par][:, :, :].bitcast(F32).rearrange("p (t k) w -> p t k w", k=2)
                link(pool.tensor_scalar(token_no[:, :], token_no[:, :], float(TOKENS), None, ALU.add))
                pool.tensor_tensor(w[:, :, 0, 1], rec_w[at.par][:, :], v[:, :, 0], ALU.mult)
                pool.tensor_tensor(w[:, :, 1, 1], e_w[:, :], v[:, :, 1], ALU.mult).then_inc(wt_ready, 1)
                wait(pool, wt_ready, upto(at), waited)
                for j in range(4):
                    n = TA if j < 2 else TB
                    pool.indirect_dma_start(slot_table, bass.IndirectOffsetOnAxis(slot[at.par][0:n, j:j + 1], 0),
                                            entry[at.par][0:n, j, :], None, bounds_check=EXPERTS * SLOTS - 1,
                                            oob_is_err=False).then_inc(slots_stored[at.par], 16)

            run(pool, [(add_bias, -1), (slots, -4), (newton1, 1), (newton2, -1)])
            for p in range(2):
                wait(pool, slots_stored[p], 64 * IMAGES // 2, waited)

        @block.tensor
        def _(pe):
            def features(at, u):
                t, q = u % 2, u // 2
                wait(pe, q_ready if q else k_ready, upto(at))
                wait(pe, feat_shifted, upto(at, 0, 4, u - 1))
                for c in range(2):
                    m = (0 if q else 2) + c
                    cols = slice(t * TA, (t + 1) * TA)
                    last = three(pe, f_ps[t][:, c, :], qk_hi[:, m, cols], qk_lo[:, m, cols], pb_hi[:, :], pb_lo[:, :], True, True)
                last.then_inc(feat_done, 1)

            def turn_four(bank, source, done):
                for k in range(KCH):
                    for t in range(2):
                        last = pe.transpose(bank[:, (k * 2 + t) * TA:(k * 2 + t + 1) * TA],
                                            source[:, t, k * 128:(k + 1) * 128], ident[0:TA, 0:TA])
                last.then_inc(done, 1)

            def turn_x(at):
                wait(pe, xn_ready, upto(at))
                turn_four(bank_d, xn[at.par], x_turned)

            def q_or_k(bank, m0, done):
                for c in range(2):
                    m = m0 + c
                    for k in range(KCH):
                        last = three(pe, bank[:, c * T2:(c + 1) * T2], wqkv_hi[:, k, m * 128:(m + 1) * 128],
                                     wqkv_lo[:, k, m * 128:(m + 1) * 128], x_hi[:, k, :], x_lo[:, k, :], k == 0, k == KCH - 1)
                last.then_inc(done, 1)

            def key(at):
                wait(pe, x_ready, upto(at))
                wait(pe, logit_ready, upto(at, -2))
                q_or_k(bank_c, 2, k_done)

            def query(at):
                wait(pe, x_ready, upto(at))
                wait(pe, attn_ready, upto(at, -1, 2, 1))
                q_or_k(bank_b, 0, q_done)

            def value(at):
                wait(pe, x_ready, upto(at))
                wait(pe, h1_ready, upto(at, -1))
                for t in range(2):
                    o = bank_c[0:TA, t * D:(t + 1) * D]
                    cols = slice(t * TA, (t + 1) * TA)
                    pe.matmul(o, one_rows[:, :], bv[:, :], start=True, stop=False)
                    for k in range(KCH):
                        last = three(pe, o, x_hi[:, k, cols], x_lo[:, k, cols],
                                     wqkv_hi[:, k, 2 * D:3 * D], wqkv_lo[:, k, 2 * D:3 * D], False, k == KCH - 1)
                last.then_inc(v_done, 1)

            def key_value(at, part):
                t, j0 = part // 2, part % 2 * (PAIRS // 2)
                wait(pe, exp_done, upto(at, 0, 4, t + 1))
                if part == 0:
                    wait(pe, v_ready, upto(at))
                n = TB if t else TA
                for j in range(j0, j0 + PAIRS // 2):
                    c = (t * PAIRS + j) * KVW
                    last = pe.matmul(bank_b[:, j * KV_MOVED:(j + 1) * KV_MOVED],
                                     feat[t][0:n, 2 * j:2 * j + 2, :].rearrange("p h f -> p (h f)"), v_flat[0:n, c:c + KV_MOVED],
                                     start=(t == 0 and j == 0), stop=(t == 1 and j == PAIRS - 1), skip_group_check=True)
                if j0:
                    last.then_inc(kv_done, 1)

            def turn_q(at, j):
                t, half = j // 2, j % 2
                wait(pe, exp_done, upto(at, 0, 4, 3 + t))
                if j == 1:
                    wait(pe, qt_ready, upto(at, 0, 4, 1))
                if j == 2:
                    wait(pe, x_ready, upto(at, 1))
                for i in range(4):
                    h = 8 * half + 2 * i
                    last = pe.transpose(qt_bank[j][:, i * TA:(i + 1) * TA],
                                        feat[2 + t][:, h:h + 2, :].rearrange("p h f -> p (h f)"), ident[0:TA, 0:TA])
                last.then_inc(q_turned, 1)

            def output(at, part):
                t, j0 = part // 2, part % 2 * (PAIRS // 2)
                wait(pe, kvb_ready, upto(at))
                wait(pe, qt_ready, upto(at, 0, 4, part + 1))
                if part == 2:
                    wait(pe, x2t_ready, upto(at, -1))
                bank = bank_a if t else bank_b
                for j in range(j0, j0 + PAIRS // 2):
                    last = pe.matmul(bank[0:TA, j * KVW:(j + O_PAIRS) * KVW], qt[2 * t + j // 4][:, j % 4, :],
                                     kvb[:, j:j + O_PAIRS, :].rearrange("p j c -> p (j c)"),
                                     start=True, stop=True)
                if j0:
                    last.then_inc(o_done, 1)

            def turn_a(at):
                wait(pe, attn_ready, upto(at, 0, 2))
                turn_four(bank_d, attn, a_turned)

            def project(at):
                wait(pe, a_ready, upto(at))
                if at.known == IMAGES - 1:
                    wait(pe, logit_ready, upto(at, -1))
                for t in range(2):
                    for k in range(KCH):
                        cols = slice(t * TA, (t + 1) * TA)
                        last = three(pe, bank_c[0:TA, t * D:(t + 1) * D], a_hi[:, k, cols], a_lo[:, k, cols],
                                     wp_hi[:, k, :], wp_lo[:, k, :], k == 0, k == KCH - 1)
                last.then_inc(proj_done, 1)

            def turn_x2(at):
                wait(pe, x2_ready, upto(at))
                wait(pe, pos_read, upto(at, -2))
                turn_four(bank_a, x2[at.par], x2_turned)

            def gate(at):
                wait(pe, x2t_ready, upto(at))
                wait(pe, qt_ready, upto(at, 1, 4))
                for t in range(2):
                    for k in range(KCH):
                        last = pe.matmul(gate_ps[0:TA, t * EXPERTS:(t + 1) * EXPERTS], x2t[:, k, t * TA:(t + 1) * TA],
                                         gw[:, k, :], start=(k == 0), stop=(k == KCH - 1))
                last.then_inc(gate_done, 1)

            def positions(at):
                wait(pe, seen_ready, upto(at))
                wait(pe, attn_ready, upto(at, 2, 2))
                if at.known == IMAGES - 1:
                    wait(pe, pos_read, upto(at, -1))
                for t in range(2):
                    o = pos_ps[0:TA, t * EXPERTS:(t + 1) * EXPERTS]
                    pe.matmul(o, before[:, :], hot_sum[at.par][:, t, :], start=True, stop=False)
                    if t == 1:
                        pe.matmul(o, ones[:, :], hot_sum[at.par][:, 0, :], start=False, stop=False)
                    last = pe.matmul(o, ones[:, :], seen[at.par][:, :], start=False, stop=True)
                last.then_inc(pos_done, 1)

            pe.wait_ge(set_up, 5)
            run(pe, [(turn_q, -1, 1), (output, -1, 0), (turn_q, -1, 2), (output, -1, 1),
                      (turn_q, -1, 3), (output, -1, 2), (gate, -2), (output, -1, 3), (key, 0),
                      (query, 0), (turn_a, -1), (positions, -3), (features, 0, 0), (project, -1),
                      (features, 0, 1), (value, 0), (features, 0, 2), (key_value, 0, 0),
                      (key_value, 0, 1), (features, 0, 3), (turn_x, 1), (key_value, 0, 2),
                      (turn_x2, -1), (key_value, 0, 3), (turn_q, 0, 0)])

        @block.scalar
        def _(act):
            def log_var(at, mv, mv_ready, lnv, lnv_ready, y0_ready):
                wait(act, mv_ready, upto(at))
                wait(act, y0_ready, upto(at, -2))
                act.activation(lnv[at.par][:, :], mv[at.par][:, :, 1], ACT.Ln, bias=ln_eps[0:TA, :]).then_inc(lnv_ready, 1)

            def root(at, lnv, lnv_ready, y0, y0_ready, scale_ready):
                wait(act, lnv_ready, upto(at))
                wait(act, scale_ready, upto(at, -2))
                act.activation(y0[at.par][:, :], lnv[at.par][:, :], ACT.Exp, scale=-0.5).then_inc(y0_ready, 1)

            def log_var1(at):
                log_var(at, mv1, mv1_ready, lnv1, lnv1_ready, y01_ready)

            def root1(at):
                root(at, lnv1, lnv1_ready, y01, y01_ready, scale1_ready)

            def log_var2(at):
                log_var(at, mv2, mv2_ready, lnv2, lnv2_ready, y02_ready)

            def root2(at):
                root(at, lnv2, lnv2_ready, y02, y02_ready, scale2_ready)

            def norm(at, src, dst, scale, shift, ready):
                for t in range(2):
                    last = act.activation(dst[at.par][:, t, :], src[at.par][:, t, :], ACT.Identity,
                                          bias=shift[at.par][:, t:t + 1], scale=scale[at.par][:, t:t + 1])
                last.then_inc(ready, 1)

            def norm1(at):
                wait(act, scale1_ready, upto(at))
                wait(act, x_turned, upto(at, -2))
                norm(at, h_in, xn, scale1, shift1, xn_ready)

            def norm2(at):
                wait(act, scale2_ready, upto(at))
                wait(act, x2_turned, upto(at, -2))
                wait(act, x2_stored[at.par], at.half * 32)
                norm(at, res, x2, scale2, shift2, x2_ready)

            def exp(at, u):
                wait(act, feat_shifted, upto(at, 0, 4, u + 1))
                f = feat[u][:, :, :].rearrange("p h f -> p (h f)")
                act.activation(f, f, ACT.Exp, bias=feat_eps[0:TA, :]).then_inc(exp_done, 1)

            def hi_x(at):
                wait(act, x_turned, upto(at))
                wait(act, v_done, upto(at, -1))
                act.activation(flat(x_hi), bank_d[:, 0:2 * T2], ACT.Copy).then_inc(x_hi_ready, 1)

            def hi_qk(at, bank, m0, done, used, ready):
                wait(act, done, upto(at))
                wait(act, feat_done, upto(at, -1, 4, used))
                for c in range(2):
                    last = act.activation(qk_hi[:, m0 + c, :], bank[:, c * T2:(c + 1) * T2], ACT.Identity,
                                          bias=bqk[:, m0 + c:m0 + c + 1])
                last.then_inc(ready, 1)

            def hi_k(at):
                hi_qk(at, bank_c, 2, k_done, 2, k_hi_ready)

            def hi_q(at):
                hi_qk(at, bank_b, 0, q_done, 4, q_hi_ready)

            def copy_v(at):
                wait(act, v_done, upto(at))
                wait(act, kv_done, upto(at, -1, 2))
                act.activation(v_ext[:, :, :, 0:2 * HEAD], bank_c[0:TA, :].rearrange("p (t j c) -> p t j c", t=2, j=PAIRS),
                               ACT.Copy).then_inc(v_ready, 1)

            def copy_qt(at, j):
                wait(act, q_turned, upto(at, 0, 4, j + 1))
                wait(act, o_done, upto(at, -1, 2, 1 + j // 2))
                act.activation(qt[j][:, :, :].rearrange("p i t -> p (i t)"), qt_bank[j][:, 0:4 * TA], ACT.Copy).then_inc(qt_ready, 1)

            def hi_a(at):
                wait(act, a_turned, upto(at))
                wait(act, proj_done, upto(at, -1))
                act.activation(flat(a_hi), bank_d[:, 0:2 * T2], ACT.Copy).then_inc(a_hi_ready, 1)

            def copy_x2t(at):
                wait(act, x2_turned, upto(at))
                wait(act, gate_done, upto(at, -1))
                act.activation(flat(x2t), bank_a[:, 0:2 * T2], ACT.Copy).then_inc(x2t_ready, 1)

            def exp_gap(at):
                wait(act, top_ready, upto(at))
                wait(act, wt_ready, upto(at, -2))
                act.activation(e_gap[at.par][:, :], gap[at.par][:, :], ACT.Exp).then_inc(e_gap_ready, 1)

            act.preload_act_table_set("natural_log_exp_and_others")
            run(act, [(copy_qt, -1, 2), (copy_qt, -1, 3), (hi_k, 0), (log_var1, 1), (root1, 1),
                      (hi_a, -1), (hi_q, 0), (norm1, 1), (exp, 0, 0), (copy_v, 0), (log_var2, -1),
                      (exp_gap, -2), (root2, -1), (exp, 0, 1), (norm2, -1), (exp, 0, 2), (hi_x, 1),
                      (copy_x2t, -1), (copy_qt, 0, 0), (exp, 0, 3), (copy_qt, 0, 1)])

        @block.vector
        def _(dve):
            def stats(at, src, stat, done, mv_ready):
                wait(dve, mv_ready, upto(at, -1))
                for t in range(2):
                    last = dve.bn_stats(stat[:, t, :], src[at.par][:, t, :])
                last.then_inc(done, 1)

            def moments(at, stat, done, mv, used, mv_ready):
                wait(dve, done, upto(at), waited)
                wait(dve, used, upto(at, -2), waited)
                for t in range(2):
                    last = dve.bn_aggr(mv[at.par][:, t, :], stat[:, t, :])
                last.then_inc(mv_ready, 1)

            def stats1(at):
                wait(dve, h_loaded[at.par], at.half * 16 + 16)
                stats(at, h_in, stat1, stat1_done, mv1_ready)

            def moments1(at):
                moments(at, stat1, stat1_done, mv1, scale1_ready, mv1_ready)

            def stats2(at):
                wait(dve, h1_ready, upto(at))
                stats(at, res, stat2, stat2_done, mv2_ready)

            def moments2(at):
                moments(at, stat2, stat2_done, mv2, scale2_ready, mv2_ready)

            def f_view(u):
                return f_ps[u % 2][:, :, :].rearrange("p c (h f) -> p (c h) f", f=FEATS)

            def maximum(at, u):
                wait(dve, feat_done, upto(at, 0, 4, u + 1))
                dve.tensor_reduce(fmax[u % 2][:, :], f_view(u), AX_X, ALU.max).then_inc(feat_maxed, 1)

            def shift(at, u):
                if u < 2:
                    wait(dve, kv_done, upto(at, -1, 2, u + 1))
                else:
                    wait(dve, q_turned, upto(at, -1, 4, 2 * u - 2))
                wait(dve, feat_maxed, upto(at, 0, 4, u + 1))
                dve.tensor_tensor(feat[u][:, :, :], f_view(u), fmax[u % 2][:, :].unsqueeze(2).to_broadcast([TA, HEADS, FEATS]),
                                  ALU.subtract).then_inc(feat_shifted, 1)

            def lo_x(at):
                wait(dve, x_hi_ready, upto(at))
                dve.tensor_tensor(flat(x_lo), bank_d[:, 0:2 * T2], flat(x_hi).bitcast(F32),
                                  ALU.subtract).then_inc(x_ready, 1)

            def lo_qk(at, bank, m0, hi_ready, ready):
                wait(dve, hi_ready, upto(at))
                for c in range(2):
                    last = dve.scalar_tensor_tensor(qk_lo[:, m0 + c, :], bank[:, c * T2:(c + 1) * T2], bqk[:, m0 + c:m0 + c + 1],
                                                    qk_hi[:, m0 + c, :].bitcast(F32), ALU.add, ALU.subtract)
                last.then_inc(ready, 1)

            def lo_k(at):
                lo_qk(at, bank_c, 2, k_hi_ready, k_ready)

            def lo_q(at):
                lo_qk(at, bank_b, 0, q_hi_ready, q_ready)

            def mask_kv(at):
                wait(dve, kv_done, upto(at, 0, 2))
                wait(dve, o_done, upto(at, -1, 2))
                dve.tensor_tensor(kvb[:, 0:PAIRS, :], bank_b[:, :].rearrange("p (j c) -> p j c", j=PAIRS)[:, :, 0:KVW],
                                  kv_mask[:, :].unsqueeze(1).to_broadcast([128, PAIRS, KVW]), ALU.mult).then_inc(kvb_ready, 1)

            def o_view(t):
                return (bank_a if t else bank_b)[0:TA, 0:PAIRS * KVW].rearrange("p (j c) -> p j c", j=PAIRS)

            def denominator(at, t):
                wait(dve, o_done, upto(at, 0, 2, t + 1))
                wait(dve, attn_ready, upto(at, -1, 2, t + 1))
                dve.tensor_scalar(den[t][:, :, :], o_view(t)[:, :, 2 * HEAD:KVW], DEN_EPS, None, ALU.add).then_inc(den_ready, 1)

            def invert(at, t):
                wait(dve, den_ready, upto(at, 0, 2, t + 1))
                dve.reciprocal(rec[t][:, :, :], den[t][:, :, :]).then_inc(rec_ready, 1)

            def normalize(at, t):
                wait(dve, rec_ready, upto(at, 0, 2, t + 1))
                wait(dve, a_turned, upto(at, -1))
                dve.tensor_tensor(attn[:, t, :].rearrange("p (j h d) -> p j h d", j=PAIRS, h=2),
                                  o_view(t)[:, :, 0:2 * HEAD].rearrange("p j (h d) -> p j h d", h=2),
                                  rec[t][:, :, :].unsqueeze(3).to_broadcast([TA, PAIRS, 2, HEAD]), ALU.mult).then_inc(attn_ready, 1)

            def lo_a(at):
                wait(dve, a_hi_ready, upto(at))
                dve.tensor_tensor(flat(a_lo), bank_d[:, 0:2 * T2], flat(a_hi).bitcast(F32), ALU.subtract).then_inc(a_ready, 1)

            def residual(at):
                wait(dve, proj_done, upto(at))
                wait(dve, res_ready, upto(at))
                r = res[at.par][:, :, :].rearrange("p t d -> p (t d)")
                dve.tensor_tensor(r, bank_c[0:TA, :], r, ALU.add).then_inc(h1_ready, 1)

            def logits(at):
                wait(dve, gate_done, upto(at))
                wait(dve, top_i_ready, upto(at, -1))
                dve.tensor_tensor(logit[:, :, :], gate_ps[0:TA, :].rearrange("p (t e) -> p t e", t=2),
                                  gb[0:TA, :, :], ALU.add).then_inc(logit_ready, 1)

            def top_values(at):
                wait(dve, logit_ready, upto(at), waited)
                wait(dve, top_ready, upto(at, -1), waited)
                for t in range(2):
                    last = dve.max(top_v[:, t, :], logit[:, t, :])
                last.then_inc(top_v_ready, 1)

            def top_experts(at):
                wait(dve, top_v_ready, upto(at), waited)
                for t in range(2):
                    last = dve.max_index(top_i[:, t, :], top_v[:, t, :], logit[:, t, :])
                last.then_inc(top_i_ready, 1)

            def numbers(at):
                wait(dve, top_i_ready, upto(at))
                wait(dve, wt_ready, upto(at, -2))
                dve.tensor_tensor(gap[at.par][:, :], top_v[:, :, 1], top_v[:, :, 0], ALU.subtract)
                dve.tensor_copy(top_no[at.par][:, :, :], top_i[:, :, 0:2]).then_inc(top_ready, 1)

            def one_hot(at):
                wait(dve, top_ready, upto(at))
                wait(dve, pos_read, upto(at, -2))
                dve.tensor_tensor(hot[at.par][:, :, :], expert_no[0:TA, :].unsqueeze(1).to_broadcast([TA, 4, EXPERTS]),
                                  top_no[at.par][:, :, :].rearrange("p t k -> p (t k)").unsqueeze(2).to_broadcast([TA, 4, EXPERTS]),
                                  ALU.is_equal).then_inc(hot_ready, 1)

            def token_hot(at):
                wait(dve, hot_ready, upto(at))
                wait(dve, pos_done, upto(at, -2))
                wait(dve, seen_ready, upto(at, -2))
                h = hot[at.par][:, :, :].rearrange("p (t k) e -> p t k e", k=2)
                dve.tensor_tensor(hot_sum[at.par][:, :, :], h[:, :, 0, :], h[:, :, 1, :], ALU.add).then_inc(hot_sum_ready, 1)

            def count_a(at):
                wait(dve, hot_sum_ready, upto(at))
                wait(dve, seen_ready, upto(at, -1))
                wait(dve, pos_done, upto(at, -1))
                dve.tensor_tensor(seen[1 - at.par][:, :], seen[at.par][:, :], hot_sum[at.par][:, 0, :], ALU.add).then_inc(seen_step, 1)

            def count_b(at):
                wait(dve, seen_step, upto(at))
                s = seen[1 - at.par]
                dve.tensor_tensor(s[0:TB, :], s[0:TB, :], hot_sum[at.par][0:TB, 1, :], ALU.add).then_inc(seen_ready, 1)

            def read_positions(at):
                wait(dve, pos_done, upto(at))
                wait(dve, placed, upto(at, -1))
                dve.tensor_tensor(prod[:, :, :].rearrange("p (t k) e -> p t k e", k=2),
                                  pos_ps[0:TA, :].rearrange("p (t e) -> p t e", t=2).unsqueeze(2).to_broadcast([TA, 2, 2, EXPERTS]),
                                  hot[at.par][:, :, :].rearrange("p (t k) e -> p t k e", k=2), ALU.mult).then_inc(pos_read, 1)

            def weight_sum(at):
                wait(dve, e_gap_ready, upto(at))
                wait(dve, placed, upto(at, -1))
                dve.tensor_scalar(den_w[:, :], e_gap[at.par][:, :], 1.0, None, ALU.add).then_inc(den_w_ready, 1)

            def place(at):
                wait(dve, pos_read, upto(at))
                wait(dve, den_w_ready, upto(at))
                wait(dve, wt_ready, upto(at, -2))
                dve.tensor_reduce(pos4[at.par][:, :], prod[:, :, :], AX_X, ALU.add)
                dve.reciprocal(rec_w[at.par][:, :], den_w[:, :]).then_inc(placed, 1)

            wait(dve, set_up, 5)
            run(dve, [(maximum, -1, 3), (shift, -1, 3), (mask_kv, -1), (lo_x, 0), (place, -4),
                      (one_hot, -3), (denominator, -1, 0), (invert, -1, 0), (token_hot, -3),
                      (count_a, -3), (weight_sum, -3), (stats1, 1), (logits, -2), (normalize, -1, 0),
                      (moments1, 1), (top_values, -2), (denominator, -1, 1), (top_experts, -2),
                      (invert, -1, 1), (count_b, -3), (normalize, -1, 1), (lo_k, 0), (lo_a, -1),
                      (lo_q, 0), (maximum, 0, 0), (residual, -1), (shift, 0, 0), (maximum, 0, 1),
                      (stats2, -1), (numbers, -2), (moments2, -1), (shift, 0, 1), (maximum, 0, 2),
                      (read_positions, -3), (shift, 0, 2)])


def experts(nc, keep, w1, w2, b2, x2_rows, sum_rows, slot_table):
    ident, b1_cols = keep["ident"], keep["b1_cols"]
    CH = 2 * FCH
    with ExitStack() as ctx:
        def sb(name, shape, dt=F32):
            return ctx.enter_context(nc.sbuf_tensor(name, shape, dt))

        def sem(name):
            return ctx.enter_context(nc.semaphore(name))

        w1_raw, w2_raw = sb("w1_raw", [128, KCH, HIDDEN]), sb("w2_raw", [128, FCH, D])
        w1_hi, w1_lo = sb("w1_hi", [128, KCH, HIDDEN], F32R), sb("w1_lo", [128, KCH, HIDDEN], F32R)
        w2_hi, w2_lo = sb("w2_hi", [128, FCH, D], F32R), sb("w2_lo", [128, FCH, D], F32R)
        b2_row = sb("b2_row", [SP, D])
        b1_col = [sb(f"b1_col{p}", [128, FCH]) for p in range(2)]
        entries = sb("entries", [SP, TJ, ENTRY], U32)
        token, source = sb("token", [SP, TJ]), sb("source", [SP, TJ], U32)
        target = [sb(f"target{p}", [SP, TJ], U32) for p in range(2)]
        spare = sb("spare", [SP, TJ])
        weight = [sb(f"weight{p}", [SP, TJ]) for p in range(2)]
        xe = sb("xe", [SP, TJ, D])
        xe_hi, xe_lo = sb("xe_hi", [128, KCH, SLOTS], F32R), sb("xe_lo", [128, KCH, SLOTS], F32R)
        act_out = [sb(f"act_out{r}", [128, HALF]) for r in range(4)]
        he_hi, he_lo = sb("he_hi", [128, 2, FCH, HALF], F32R), sb("he_lo", [128, 2, FCH, HALF], F32R)
        y_bias = [sb(f"y_bias{r}", [SP, 2, D]) for r in range(2)]
        y_sb = sb("y_sb", [SP, TJ, D])
        u_ps = [ctx.enter_context(nc.psum_tensor(f"u_ps{r}", [128, 512], F32)) for r in range(4)]
        y_ps = [ctx.enter_context(nc.psum_tensor(f"y_ps{r}", [SP, 2, D], F32)) for r in range(2)]
        x_ps = [ctx.enter_context(nc.psum_tensor(f"x_ps{r}", [128, 512], F32)) for r in range(2)]

        w1_loaded, w2_loaded, b2_loaded, table_loaded = sem("w1_loaded"), sem("w2_loaded"), sem("b2_loaded"), sem("table_loaded")
        w1_hi_ready, w1_ready, w2_hi_ready, w2_ready = sem("w1_hi_ready"), sem("w1_ready"), sem("w2_hi_ready"), sem("w2_ready")
        index_step, source_ready, gathered, scattered = sem("index_step"), sem("source_ready"), sem("gathered"), sem("scattered")
        xe_turned, xe_hi_ready, xe_ready = sem("xe_turned"), sem("xe_hi_ready"), sem("xe_ready")
        b1_ready, up_done, gelu_done, he_hi_done, he_ready = (
            sem("b1_ready"), sem("up_done"), sem("gelu_done"), sem("he_hi_done"), sem("he_ready"))
        down_done, y_biased, y_ready, spare_ready = sem("down_done"), sem("y_biased"), sem("y_ready"), sem("spare_ready")
        waited = sem("waited")
        block = ctx.enter_context(nc.Block())

        def of(dram, e):
            return dram[e] if isinstance(e, int) else dram[bass.ds(e, 1)]

        def run(eng, first, turn):
            first()
            for e in range(2):
                turn(e, e, True)
            with eng.Fori(1, EXPERTS // 2 - 1) as it:
                for p in range(2):
                    turn(it * 2 + p, p, True)
            turn(EXPERTS - 2, 0, True)
            turn(EXPERTS - 1, 1, False)

        w1_v = w1.rearrange("e (k p) f -> e p k f", p=128)
        w2_v = w2.rearrange("e (c p) d -> e p c d", p=128)
        table_v = slot_table.rearrange("(e p j) w -> e p j w", p=SP, j=TJ)

        @block.sync
        def _(sp):
            def squeeze(ap, e):
                return ap if isinstance(e, int) else ap.rearrange("a p k f -> (a p) k f")

            def load_w1(e):
                wait(sp, w1_ready, e * 2, waited)
                sp.dma_start(w1_raw[:, :, :], squeeze(of(w1_v, e), e)).then_inc(w1_loaded, 16)

            def load_w2(e):
                wait(sp, w2_ready, e * 2, waited)
                sp.dma_start(w2_raw[:, :, :], squeeze(of(w2_v, e), e)).then_inc(w2_loaded, 16)

            def load_table(e):
                wait(sp, source_ready, e, waited)
                sp.dma_start(entries[:, :, :], squeeze(of(table_v, e), e)).then_inc(table_loaded, 16)

            def load_b2(e):
                wait(sp, y_biased, e * 4, waited)
                row = b2[e] if isinstance(e, int) else b2[bass.ds(e, 1), :].rearrange("a d -> (a d)")
                sp.dma_start(b2_row[:, :], row.partition_broadcast(SP)).then_inc(b2_loaded, 16)

            def first():
                load_table(0)
                load_w1(0)
                sp.wait_ge(gathered, 16 * TJ)
                load_w2(0)

            def turn(e, p, more):
                load_b2(e)
                if more:
                    load_w1(e + 1)
                    load_table(e + 1)
                    load_w2(e + 1)

            run(sp, first, turn)

        @block.gpsimd
        def _(pool):
            def gather(e):
                wait(pool, source_ready, e + 1, waited)
                wait(pool, xe_turned, e * 4, waited)
                for j in range(TJ):
                    pool.indirect_dma_start(xe[:, j, :], None, x2_rows, bass.IndirectOffsetOnAxis(source[:, j:j + 1], 0))\
                        .then_inc(gathered, 16)

            def scatter(e, p):
                wait(pool, scattered, e * (16 * TJ), waited)
                for j in range(TJ):
                    if j % 2 == 0:
                        wait(pool, y_ready, e * 4 + j // 2 + 1, waited)
                    pool.indirect_dma_start(sum_rows, bass.IndirectOffsetOnAxis(target[p][:, j:j + 1], 0), y_sb[:, j, :], None,
                                            compute_op=ALU.add).then_inc(scattered, 16)

            def turn(e, p, more):
                if more:
                    gather(e + 1)
                scatter(e, p)

            pool.iota(spare[:, :], pattern=[[1, TJ]], base=ROWS, channel_multiplier=TJ,
                      allow_small_or_imprecise_dtypes=True).then_inc(spare_ready, 1)
            run(pool, lambda: gather(0), turn)
            wait(pool, scattered, EXPERTS * TJ * 16, waited)

        @block.tensor
        def _(pe):
            def turn_x(e, i):
                half, k = i // 2, i % 2
                if i == 0:
                    pe.wait_ge(gathered, e * (16 * TJ) + 16 * TJ)
                wait(pe, xe_ready, e * 4 + i - 1)
                for j in range(4):
                    last = pe.transpose(x_ps[i % 2][:, j * SP:(j + 1) * SP], xe[:, half * 4 + j, k * 128:(k + 1) * 128],
                                        ident[0:SP, 0:SP])
                last.then_inc(xe_turned, 1)

            def up(e, i):
                half, c = i // FCH, i % FCH
                if i == 0:
                    pe.wait_ge(w1_ready, e * 2 + 2)
                if c == 0:
                    pe.wait_ge(xe_ready, e * 4 + 2 * half + 2)
                wait(pe, gelu_done, e * CH + i - 3)
                for k in range(KCH):
                    last = three(pe, u_ps[i % 4][:, 0:HALF], w1_hi[:, k, c * 128:(c + 1) * 128],
                                 w1_lo[:, k, c * 128:(c + 1) * 128], xe_hi[:, k, half * HALF:(half + 1) * HALF],
                                 xe_lo[:, k, half * HALF:(half + 1) * HALF], k == 0, k == KCH - 1)
                last.then_inc(up_done, 1)

            def down(e, i):
                half = i // 2
                if i == 0:
                    pe.wait_ge(w2_ready, e * 2 + 2)
                if i % 2 == 0:
                    pe.wait_ge(he_ready, e * CH + (half + 1) * FCH)
                wait(pe, y_biased, e * 4 + i - 1)
                for j in range(2):
                    cols = slice((i % 2 * 2 + j) * SP, (i % 2 * 2 + j + 1) * SP)
                    for c in range(FCH):
                        last = three(pe, y_ps[i % 2][:, j, :], he_hi[:, half, c, cols], he_lo[:, half, c, cols],
                                     w2_hi[:, c, :], w2_lo[:, c, :], c == 0, c == FCH - 1)
                last.then_inc(down_done, 1)

            def turn(e, p, more):
                for i in range(CH):
                    up(e, i)
                for i in range(4):
                    down(e, i)
                    if more and i < 2:
                        turn_x(e + 1, 2 * i)
                        turn_x(e + 1, 2 * i + 1)

            run(pe, lambda: [turn_x(0, i) for i in range(4)], turn)

        @block.scalar
        def _(act):
            def hi_w1(e, k):
                act.wait_ge(w1_loaded, e * 16 + 16)
                wait(act, up_done, e * CH)
                act.activation(w1_hi[:, k, :], w1_raw[:, k, :], ACT.Copy).then_inc(w1_hi_ready, 1)

            def hi_w2(e, k):
                act.wait_ge(w2_loaded, e * 16 + 16)
                wait(act, down_done, e * 4)
                act.activation(w2_hi[:, 4 * k:4 * k + 4, :], w2_raw[:, 4 * k:4 * k + 4, :], ACT.Copy).then_inc(w2_hi_ready, 1)

            def hi_x(e, i):
                half, k = i // 2, i % 2
                act.wait_ge(xe_turned, e * 4 + i + 1)
                wait(act, up_done, e * CH)
                act.activation(xe_hi[:, k, half * HALF:(half + 1) * HALF], x_ps[i % 2][:, 0:HALF], ACT.Copy).then_inc(xe_hi_ready, 1)

            def bias(e, p):
                col = b1_cols[:, e, :] if isinstance(e, int) else b1_cols[:, bass.ds(e, 1), :].rearrange("p a c -> p (a c)")
                act.activation(b1_col[p][:, :], col, ACT.Copy).then_inc(b1_ready, 1)

            def gelu(e, p, i):
                if i == 0:
                    act.wait_ge(b1_ready, e + 1)
                act.wait_ge(up_done, e * CH + i + 1)
                wait(act, he_ready, e * CH + i - 3)
                act.activation(act_out[i % 4][:, :], u_ps[i % 4][:, 0:HALF], ACT.Gelu,
                               bias=b1_col[p][:, i % FCH:i % FCH + 1]).then_inc(gelu_done, 1)

            def weigh(e, p, i):
                act.wait_ge(y_biased, e * 4 + i + 1)
                if i == 0:
                    wait(act, scattered, e * (16 * TJ))
                for j in range(2):
                    last = act.activation(y_sb[:, 2 * i + j, :], y_bias[i % 2][:, j, :], ACT.Copy,
                                          scale=weight[p][:, 2 * i + j:2 * i + j + 1])
                last.then_inc(y_ready, 1)

            def first():
                for k in range(2):
                    hi_w1(0, k)
                for i in range(4):
                    hi_x(0, i)
                bias(0, 0)

            def turn(e, p, more):
                for i in range(CH):
                    gelu(e, p, i)
                    if i in (1, 5):
                        hi_w2(e, i // 4)
                if more:
                    bias(e + 1, 1 - p)
                    hi_w1(e + 1, 0)
                    hi_x(e + 1, 0)
                    hi_x(e + 1, 1)
                weigh(e, p, 0)
                if more:
                    hi_w1(e + 1, 1)
                    hi_x(e + 1, 2)
                    hi_x(e + 1, 3)
                for i in range(1, 4):
                    weigh(e, p, i)

            run(act, first, turn)

        @block.vector
        def _(dve):
            def lo_w1(e, k):
                dve.wait_ge(w1_hi_ready, e * 2 + k + 1)
                dve.tensor_tensor(w1_lo[:, k, :], w1_raw[:, k, :], w1_hi[:, k, :].bitcast(F32), ALU.subtract).then_inc(w1_ready, 1)

            def lo_w2(e, k):
                c = slice(4 * k, 4 * k + 4)
                dve.wait_ge(w2_hi_ready, e * 2 + k + 1)
                dve.tensor_tensor(w2_lo[:, c, :], w2_raw[:, c, :], w2_hi[:, c, :].bitcast(F32), ALU.subtract).then_inc(w2_ready, 1)

            def lo_x(e, i):
                half, k = i // 2, i % 2
                cols = slice(half * HALF, (half + 1) * HALF)
                dve.wait_ge(xe_hi_ready, e * 4 + i + 1)
                dve.tensor_tensor(xe_lo[:, k, cols], x_ps[i % 2][:, 0:HALF], xe_hi[:, k, cols].bitcast(F32),
                                  ALU.subtract).then_inc(xe_ready, 1)

            def index(e, p):
                dve.wait_ge(table_loaded, e * 16 + 16)
                wait(dve, gathered, e * (16 * TJ))
                dve.tensor_copy(token[:, :], entries[:, :, 0]).then_inc(index_step, 1)
                dve.wait_ge(index_step, e + 1)
                dve.tensor_scalar(source[:, :], token[:, :], float(ROWS - 1), None, ALU.min)
                wait(dve, scattered, (e - 1) * (16 * TJ))
                dve.tensor_tensor(target[p][:, :], token[:, :], spare[:, :], ALU.min)
                dve.tensor_copy(weight[p][:, :], entries[:, :, 1].bitcast(F32)).then_inc(source_ready, 1)

            def split(e, i):
                half, c = i // FCH, i % FCH
                if c == 0:
                    wait(dve, down_done, e * 4 - 2 + 2 * half)
                dve.wait_ge(gelu_done, e * CH + i + 1)
                dve.tensor_copy(he_hi[:, half, c, :], act_out[i % 4][:, :]).then_inc(he_hi_done, 1)
                dve.wait_ge(he_hi_done, e * CH + i + 1)
                dve.tensor_tensor(he_lo[:, half, c, :], act_out[i % 4][:, :], he_hi[:, half, c, :].bitcast(F32),
                                  ALU.subtract).then_inc(he_ready, 1)

            def bias(e, i):
                if i == 0:
                    dve.wait_ge(b2_loaded, e * 16 + 16)
                wait(dve, y_ready, e * 4 + i - 1)
                dve.wait_ge(down_done, e * 4 + i + 1)
                dve.tensor_tensor(y_bias[i % 2][:, :, :], y_ps[i % 2][:, :, :],
                                  b2_row[:, :].unsqueeze(1).to_broadcast([SP, 2, D]), ALU.add).then_inc(y_biased, 1)

            def first():
                dve.wait_ge(spare_ready, 1)
                index(0, 0)
                for k in range(2):
                    lo_w1(0, k)
                for i in range(4):
                    lo_x(0, i)

            def turn(e, p, more):
                for i in range(CH):
                    split(e, i)
                    if i in (1, 5):
                        lo_w2(e, i // 4)
                    if i == 3 and more:
                        index(e + 1, 1 - p)
                bias(e, 0)
                if more:
                    lo_w1(e + 1, 0)
                    lo_x(e + 1, 0)
                    lo_x(e + 1, 1)
                bias(e, 1)
                if more:
                    lo_w1(e + 1, 1)
                    lo_x(e + 1, 2)
                    lo_x(e + 1, 3)
                bias(e, 2)
                bias(e, 3)

            run(dve, first, turn)


def finish(nc, sum_rows, out):
    PARTS = 4
    with ExitStack() as ctx:
        copied = ctx.enter_context(nc.semaphore("copied"))
        block = ctx.enter_context(nc.Block())
        out_f = out.rearrange("i n d -> (i n) d")

        @block.sync
        def _(sp):
            for i in range(PARTS):
                r = slice(ROWS // PARTS * i, ROWS // PARTS * (i + 1))
                sp.dma_start(out_f[r, :], sum_rows[r, :]).then_inc(copied, 16)
            sp.wait_ge(copied, 16 * PARTS)


_INS = ['x', 'cls_tok', 'L0_tok_W_embed', 'L0_tok_b_embed', 'L0_tok_pos_embed', 'L0_attn_W_qkv', 'L0_attn_b_qkv',
        'L0_attn_W_proj', 'L0_attn_b_proj', 'L0_attn_proj_mat', 'L0_ffn_gate_w', 'L0_ffn_gate_b', 'L0_ffn_w1',
        'L0_ffn_b1', 'L0_ffn_w2', 'L0_ffn_b2']
_OUTS = [((IMAGES, TOKENS, D), 'float32')]


def kernel(**inputs):
    import numpy as _np
    import concourse.bacc as _bacc
    from concourse import mybir as _mybir
    from concourse.bass_utils import run_bass_kernel_spmd as _run

    nc = _bacc.Bacc("TRN2", target_bir_lowering=False, num_devices=1)
    arrays, args = {}, []
    for name in _INS:
        a = _np.ascontiguousarray(inputs[name])
        arrays[f"in_{name}_dram"] = a
        args.append(nc.dram_tensor(f"in_{name}_dram", a.shape, _mybir.dt.from_np(a.dtype), kind="ExternalInput").ap())
    for i, (shape, dtype) in enumerate(_OUTS):
        dt = _mybir.dt.from_np(_np.dtype(dtype))
        args.append(nc.dram_tensor(f"out_{i}_dram", shape, dt, kind="ExternalOutput").ap())
    tower_kernel(nc, *args)
    r = _run(nc, [arrays], core_ids=[0])
    got = tuple(r.results[0][f"out_{i}_dram"] for i in range(len(_OUTS)))
    return got[0]
```
